# Optimizing a Trainium2 kernel written in Bass

```python
import numpy as np
import jax
import jax.numpy as jnp

def _softmax(x, axis=-1):
    return jax.nn.softmax(x, axis=axis)

def _gelu(x):
    return jax.nn.gelu(x, approximate=True)

def _silu(x):
    return jax.nn.silu(x)

def _sigmoid(x):
    return jax.nn.sigmoid(x)

def _layernorm(x, axis=-1, eps=1e-05):
    m = jnp.mean(x, axis=axis, keepdims=True)
    v = jnp.var(x, axis=axis, keepdims=True)
    return (x - m) / jnp.sqrt(v + eps)

def _scatter_add(tgt, idx, src, axis=0):
    return tgt.at[idx].add(src)

def _segment_sum(src, seg, n):
    return jax.ops.segment_sum(src, seg, n)
kernel_name = 'mk_hybrid_d1_jaxref_r8_8b538b'

def setup_inputs(seed: int=0):
    np.random.seed(seed)
    _w = jnp.asarray

    def _L0_attn_a_setup():
        import jax, jax.numpy as jnp
        import numpy as np
        B, T, C = (8, 256, 128)
        key = jax.random.key(seed)
        ks = jax.random.split(key, 5)
        x = jax.random.normal(ks[0], (B, T, C), dtype=jnp.float32)
        Wq = jax.random.normal(ks[1], (C, C), dtype=jnp.float32) * 0.01
        Wk = jax.random.normal(ks[2], (C, C), dtype=jnp.float32) * 0.01
        Wv = jax.random.normal(ks[3], (C, C), dtype=jnp.float32) * 0.01
        Wo = jax.random.normal(ks[4], (C, C), dtype=jnp.float32) * 0.01
        bo = jnp.zeros((C,), dtype=jnp.float32)
        return {'x': x, 'Wq': Wq, 'Wk': Wk, 'Wv': Wv, 'Wo': Wo, 'bo': bo}
    _L0_attn_a_in = _L0_attn_a_setup()

    def _L0_attn_b_setup():
        import jax, jax.numpy as jnp
        import numpy as np
        D_MODEL = 128
        N_HEADS = 16
        D_K = D_MODEL // N_HEADS
        key = jax.random.key(seed)
        ks = jax.random.split(key, 11)
        s = 1.0 / np.sqrt(D_MODEL)
        x = jax.random.normal(ks[0], (2, 256, D_MODEL), dtype=jnp.float32)
        Wq = jax.random.uniform(ks[1], (D_MODEL, D_MODEL), jnp.float32, -s, s)
        bq = jax.random.uniform(ks[2], (D_MODEL,), jnp.float32, -s, s)
        Wk = jax.random.uniform(ks[3], (D_MODEL, D_MODEL), jnp.float32, -s, s)
        bk = jax.random.uniform(ks[4], (D_MODEL,), jnp.float32, -s, s)
        Wv = jax.random.uniform(ks[5], (D_MODEL, D_MODEL), jnp.float32, -s, s)
        bv = jax.random.uniform(ks[6], (D_MODEL,), jnp.float32, -s, s)
        Wo = jax.random.uniform(ks[7], (D_MODEL, D_MODEL), jnp.float32, -s, s)
        bo = jax.random.uniform(ks[8], (D_MODEL,), jnp.float32, -s, s)
        gamma = jnp.ones((D_MODEL,), jnp.float32)
        beta = jnp.zeros((D_MODEL,), jnp.float32)
        return {'x': x, 'Wq': Wq, 'bq': bq, 'Wk': Wk, 'bk': bk, 'Wv': Wv, 'bv': bv, 'Wo': Wo, 'bo': bo, 'gamma': gamma, 'beta': beta}
    _L0_attn_b_in = _L0_attn_b_setup()

    def _L0_ffn_setup():
        import jax, jax.numpy as jnp
        import numpy as np
        B, S, DIM, FFN, E = (4, 256, 128, 512, 8)
        key = jax.random.key(seed)
        k0, k1, k2, k3 = jax.random.split(key, 4)
        scale = 0.02
        return {'hidden_states': jax.random.normal(k0, (B, S, DIM), jnp.float32), 'router_w': jax.random.normal(k1, (DIM, E), jnp.float32) * scale, 'router_b': jnp.zeros((E,), jnp.float32), 'w1': jax.random.normal(k2, (E, DIM, 2 * FFN), jnp.float32) * scale, 'w2': jax.random.normal(k3, (E, FFN, DIM), jnp.float32) * scale}
    _L0_ffn_in = _L0_ffn_setup()
    _d = {'L0_attn_a_x': _L0_attn_a_in['x'], 'L0_attn_a_Wq': _L0_attn_a_in['Wq'], 'L0_attn_a_Wk': _L0_attn_a_in['Wk'], 'L0_attn_a_Wv': _L0_attn_a_in['Wv'], 'L0_attn_a_Wo': _L0_attn_a_in['Wo'], 'L0_attn_a_bo': _L0_attn_a_in['bo'], 'L0_attn_b_Wq': _L0_attn_b_in['Wq'], 'L0_attn_b_bq': _L0_attn_b_in['bq'], 'L0_attn_b_Wk': _L0_attn_b_in['Wk'], 'L0_attn_b_bk': _L0_attn_b_in['bk'], 'L0_attn_b_Wv': _L0_attn_b_in['Wv'], 'L0_attn_b_bv': _L0_attn_b_in['bv'], 'L0_attn_b_Wo': _L0_attn_b_in['Wo'], 'L0_attn_b_bo': _L0_attn_b_in['bo'], 'L0_attn_b_gamma': _L0_attn_b_in['gamma'], 'L0_attn_b_beta': _L0_attn_b_in['beta'], 'L0_ffn_router_w': _L0_ffn_in['router_w'], 'L0_ffn_router_b': _L0_ffn_in['router_b'], 'L0_ffn_w1': _L0_ffn_in['w1'], 'L0_ffn_w2': _L0_ffn_in['w2']}
    _x0 = _d['L0_attn_a_x']
    _d['L0_attn_a_x'] = jax.random.normal(jax.random.fold_in(jax.random.key(seed), 1), (2, 1024, 128), dtype=_x0.dtype)
    del _x0
    return _d

def reference(L0_attn_a_x, L0_attn_a_Wq, L0_attn_a_Wk, L0_attn_a_Wv, L0_attn_a_Wo, L0_attn_a_bo, L0_attn_b_Wq, L0_attn_b_bq, L0_attn_b_Wk, L0_attn_b_bk, L0_attn_b_Wv, L0_attn_b_bv, L0_attn_b_Wo, L0_attn_b_bo, L0_attn_b_gamma, L0_attn_b_beta, L0_ffn_router_w, L0_ffn_router_b, L0_ffn_w1, L0_ffn_w2):

    def _L0_attn_a_ref(x, Wq, Wk, Wv, Wo, bo):
        import jax, jax.numpy as jnp
        import numpy as np
        B, T, C = (8, 256, 128)
        Bn, Tn, Cn = x.shape
        q = jnp.einsum('btc,dc->btd', x, Wq) * 0.1
        k = jnp.einsum('btc,dc->btd', x, Wk) * 0.1
        v = jnp.einsum('btc,dc->btd', x, Wv)
        att = jnp.einsum('bqd,bkd->bqk', q, k)
        rows = jnp.arange(Tn)
        mask = (rows[:, None] >= rows[None, :]).astype(x.dtype)
        att = att * mask - (1.0 - mask)
        att = att / (jnp.sum(att, axis=-1, keepdims=True) + 1e-05)
        y = jnp.einsum('bqk,bkd->bqd', att, v)
        y = jnp.einsum('btc,dc->btd', y, Wo) + bo
        return y

    def _L0_attn_b_ref(x, Wq, bq, Wk, bk, Wv, bv, Wo, bo, gamma, beta):
        import jax, jax.numpy as jnp
        import numpy as np
        D_MODEL = 128
        N_HEADS = 16
        D_K = D_MODEL // N_HEADS
        B, S, D = x.shape
        q = (x @ Wq + bq).reshape(B, S, N_HEADS, D_K).transpose(0, 2, 1, 3)
        k = (x @ Wk + bk).reshape(B, S, N_HEADS, D_K).transpose(0, 2, 1, 3)
        v = (x @ Wv + bv).reshape(B, S, N_HEADS, D_K).transpose(0, 2, 1, 3)
        scale = 1.0 / jnp.sqrt(jnp.float32(D_K))
        scores = jnp.einsum('bhqd,bhkd->bhqk', q, k) * scale
        attn = jax.nn.softmax(scores, axis=-1)
        context = jnp.einsum('bhqk,bhkd->bhqd', attn, v)
        context = context.transpose(0, 2, 1, 3).reshape(B, S, D)
        output = context @ Wo + bo
        y = x + output
        mu = jnp.mean(y, axis=-1, keepdims=True)
        var = jnp.mean(jnp.square(y - mu), axis=-1, keepdims=True)
        return (y - mu) * jax.lax.rsqrt(var + 1e-05) * gamma + beta

    def _L0_ffn_ref(hidden_states, router_w, router_b, w1, w2):
        import jax, jax.numpy as jnp
        import numpy as np
        B, S, DIM, FFN, E = (4, 256, 128, 512, 8)
        b, s, d = hidden_states.shape
        x = hidden_states.reshape(-1, d)
        logits = x @ router_w + router_b
        route = jax.nn.softmax(logits, axis=1)
        max_prob = jnp.max(route, axis=1, keepdims=True)
        max_ind = jnp.argmax(route, axis=1)
        out = jnp.zeros_like(x)
        num_experts = w1.shape[0]
        for e in range(num_experts):
            h = x @ w1[e]
            a, g = jnp.split(h, 2, axis=1)
            y = jax.nn.silu(a) * g @ w2[e]
            out = jnp.where((max_ind == e)[:, None], y, out)
        out = out * max_prob
        return out.reshape(b, s, d)
    x = L0_attn_a_x
    x = x + _L0_attn_a_ref(_layernorm(x, axis=-1), L0_attn_a_Wq, L0_attn_a_Wk, L0_attn_a_Wv, L0_attn_a_Wo, L0_attn_a_bo)
    x = x + _L0_ffn_ref(_layernorm(x, axis=-1), L0_ffn_router_w, L0_ffn_router_b, L0_ffn_w1, L0_ffn_w2)
    x = x + _L0_attn_b_ref(_layernorm(x, axis=-1), L0_attn_b_Wq, L0_attn_b_bq, L0_attn_b_Wk, L0_attn_b_bk, L0_attn_b_Wv, L0_attn_b_bv, L0_attn_b_Wo, L0_attn_b_bo, L0_attn_b_gamma, L0_attn_b_beta)
    x = x + _L0_ffn_ref(_layernorm(x, axis=-1), L0_ffn_router_w, L0_ffn_router_b, L0_ffn_w1, L0_ffn_w2)
    return x

_drawn_inputs = setup_inputs


def setup_inputs(seed=0):
    import zlib

    import numpy as np

    out = dict(_drawn_inputs(seed))
    spreads = {'L0_attn_a_bo': (0.0, 0.1),
     'L0_attn_b_gamma': (1.0, 0.2),
     'L0_attn_b_beta': (0.0, 0.1),
     'L0_ffn_router_b': (0.0, 0.8)}
    factors = {'L0_attn_a_Wq': 8.0,
     'L0_attn_a_Wk': 7.315,
     'L0_attn_a_Wv': 8.0,
     'L0_attn_a_Wo': 8.0,
     'L0_attn_b_Wq': 8.0,
     'L0_attn_b_bq': 8.0,
     'L0_attn_b_Wk': 8.0,
     'L0_attn_b_bk': 8.0,
     'L0_attn_b_Wv': 3.238,
     'L0_attn_b_bv': 3.436,
     'L0_ffn_router_w': 8.0,
     'L0_ffn_w1': 8.0,
     'L0_ffn_w2': 8.0}
    for name, (base, spread) in spreads.items():
        noise = np.random.default_rng([zlib.crc32(name.encode()), seed]).standard_normal(out[name].shape)
        drawn = base * np.exp(spread * noise) if base else spread * noise
        out[name] = jnp.asarray(drawn.astype(out[name].dtype))
    for name, factor in factors.items():
        out[name] = (out[name] * factor).astype(out[name].dtype)
    return out
```

```python
from contextlib import ExitStack

import concourse.bass as bass
from concourse import mybir

F32 = mybir.dt.float32
BF16 = mybir.dt.bfloat16
I32 = mybir.dt.int32
ACT = mybir.ActivationFunctionType
ALU = mybir.AluOpType
AX_X = mybir.AxisListType.X

P = 128
BATCH, SEQ = 2, 1024
NT = BATCH * SEQ // P
CH = SEQ // P
LN_EPS = 1e-5
EXPERTS, FFN = 8, 512
FJ = FFN // P
BLOCKS = NT + EXPERTS - 1
HEADS, DK = 16, 8
HG = 4
QH = 512
PARTS = 3
PRODUCTS = [(0, 0), (0, 1), (1, 0), (0, 2), (1, 1), (2, 0)]
SHIFT_ROW = 4 * DK
ROWS = len(PRODUCTS) * DK + PARTS
PROW = [n * DK if n < 4 else n * DK + PARTS for n in range(len(PRODUCTS))]
SCALE = (1.0 / DK) ** 0.5
HGROUPS = HEADS // HG
UNITS = BATCH * SEQ // QH
KT = SEQ // P
QT = QH // P


def constants():
    import numpy as np
    p = np.arange(P)
    e = np.arange(EXPERTS)
    rows = [
        np.eye(P),
        (p[:, None] < p[None, :]),
        np.tile(EXPERTS - e, (P, 1)),
        np.tile(P * np.arange(NT), (P, 1)),
        np.tile((e[None, :] <= e[:, None]).reshape(1, -1), (P, 1)),
        np.tile(np.arange(BLOCKS), (P, 1)),
    ]
    return np.ascontiguousarray(np.concatenate(rows, axis=1).astype(np.float32))


CONST_COLS = 2 * P + EXPERTS + NT + EXPERTS * EXPERTS + BLOCKS


def hybrid_layer(nc, x, a_wq, a_wk, a_wv, a_wo, a_bo, b_wq, b_bq, b_wk, b_bk, b_wv, b_bv, b_wo, b_bo,
                 b_gamma, b_beta, router_w, router_b, w1, w2, consts, out):
    with ExitStack() as ctx:
        def sb(name, shape, dt=F32):
            return ctx.enter_context(nc.sbuf_tensor(name, shape, dt))

        scope = [ctx]
        used = []

        def sem(name):
            used.append(scope[-1].enter_context(nc.semaphore(name)))
            return used[-1]

        def own(stack):
            return lambda name, shape, dt=F32: stack.enter_context(nc.sbuf_tensor(name, shape, dt))

        def dram(name, shape, dt):
            return nc.dram_tensor(name, shape, dt, kind="Internal").ap()

        psum = ctx.enter_context(nc.psum_tensor("psum", [P, 8, 512], F32))
        banks = [psum[:, n, :] for n in range(8)]

        X = sb("X", [P, NT, P])
        H = sb("H", [P, NT, P])
        work = sb("work", [P, NT, P])
        tab = sb("tab", [P, CONST_COLS])
        ident = tab[:, 0:P]
        before = tab[:, P:2 * P]
        at = 2 * P
        rank_rev = tab[:, at:at + EXPERTS]
        at += EXPERTS
        thresholds = tab[:, at:at + NT]
        at += NT
        upto = tab[:, at:at + EXPERTS * EXPERTS]
        at += EXPERTS * EXPERTS
        block_no = tab[:, at:at + BLOCKS]
        ident_bf = sb("ident_bf", [P, P], BF16)
        before_bf = sb("before_bf", [P, P], BF16)
        ones_bf = sb("ones_bf", [P, P], BF16)
        neg_ones = sb("neg_ones", [P, P])
        w1_sb = sb("w1_sb", [P, EXPERTS, 2 * FFN])
        w2_sb = sb("w2_sb", [P, EXPERTS, FJ, P])
        rw_sb = sb("rw_sb", [P, EXPERTS])
        rb_sb = sb("rb_sb", [P, EXPERTS])
        abo_sb = sb("abo_sb", [P, P])
        bw_sb = sb("bw_sb", [P, 4, P])
        bcol = sb("bcol", [P, 2])
        brow = sb("brow", [P, 4, P])
        stats = sb("stats", [P, NT, 6])
        mean = sb("mean", [P, NT])
        var = sb("var", [P, NT])
        rstd = sb("rstd", [P, NT])
        ln_a = sb("ln_a", [P, NT])
        ln_b = sb("ln_b", [P, NT])
        const_in = sem("const_in")
        w1_in, w2_in, bw_in = sem("w1_in"), sem("w2_in"), sem("bw_in")
        pad_in = sem("pad_in")
        scattered = sem("scattered")
        gathered = [sem(f"gathered{g}") for g in range(4)]

        slots_dram = dram("slots", [BLOCKS * P, P], F32)
        ys_dram = dram("ys", [BLOCKS * P, P], F32)
        qd = dram("q_stack", [BATCH * HEADS, ROWS, SEQ], BF16)
        kd = dram("k_stack", [BATCH * HEADS, ROWS, SEQ], BF16)

        def tile_of(t, i):
            return t[:, bass.ds(i, 1), :].rearrange("p a b -> p (a b)")

        def linker(eng, done):
            count = [0]

            def link(ins):
                count[0] += 1
                ins.then_inc(done, 1)
                eng.wait_ge(done, count[0])
            return link

        def norm_stats(dve, link, src, stats_done, var_ready, std_ready):
            with dve.Fori(0, NT // 4) as i:
                for k in range(4):
                    dve.bn_stats(stats[:, bass.ds(i * 4 + k, 1), :].rearrange("p a b -> p (a b)"),
                                 tile_of(src, i * 4 + k)).then_inc(stats_done, 1)
            dve.wait_ge(stats_done, NT)
            link(dve.tensor_tensor(mean[:], stats[:, :, 1], stats[:, :, 4], ALU.add))
            link(dve.tensor_scalar(mean[:], mean[:], 0.5, None, ALU.mult))
            link(dve.tensor_tensor(ln_a[:], stats[:, :, 1], stats[:, :, 4], ALU.subtract))
            link(dve.scalar_tensor_tensor(ln_a[:], ln_a[:], 0.25, ln_a[:], ALU.mult, ALU.mult))
            link(dve.tensor_tensor(ln_b[:], stats[:, :, 2], stats[:, :, 5], ALU.add))
            link(dve.scalar_tensor_tensor(var[:], ln_b[:], 1.0 / P, ln_a[:], ALU.mult, ALU.add))
            dve.tensor_scalar(var[:], var[:], LN_EPS, None, ALU.add).then_inc(var_ready, 1)
            dve.wait_ge(std_ready, 1)
            link(dve.reciprocal(rstd[:], ln_a[:]))
            link(dve.tensor_tensor(ln_b[:], rstd[:], rstd[:], ALU.mult))
            link(dve.tensor_tensor(ln_b[:], ln_b[:], var[:], ALU.mult))
            link(dve.tensor_scalar(ln_b[:], ln_b[:], -0.5, 1.5, ALU.mult, ALU.add))
            link(dve.tensor_tensor(rstd[:], rstd[:], ln_b[:], ALU.mult))

        def norm_sqrt(act, var_ready, std_ready):
            act.wait_ge(var_ready, 1)
            act.activation(ln_a[:], var[:], ACT.Sqrt).then_inc(std_ready, 1)

        def normed(dve, dst, src, t):
            return dve.tensor_scalar(dst, src, mean[:, t:t + 1], rstd[:, t:t + 1], ALU.subtract, ALU.mult)

        def linear_attention(sb):
            VX = P + 1
            aw = sb("aw", [P, 4, P])
            woT = sb("woT", [P, P])
            gmat = sb("gmat", [P, P])
            vmat = sb("vmat", [P, P])
            hn = sb("hn", [P, BATCH, P])
            hT = sb("hT_a", [P, BATCH, P])
            gT = sb("gT", [P, BATCH, P])
            vx = sb("vx", [P, BATCH, VX])
            keep = sb("keep", [P, P])
            keep_less_1 = sb("keep_less_1", [P, P])
            sT = sb("sT", [P, BATCH, P])
            sTm = sb("sTm", [P, BATCH, P])
            state = sb("state", [P, BATCH, VX])
            acc = sb("acc", [P, BATCH, CH, VX])
            tail = sb("tail", [P, BATCH, CH, VX])
            later = sb("later", [P, BATCH, CH, VX])
            rden = sb("rden", [P, NT])
            x_in, aw_in = sem("a_x_in"), sem("a_w_in")
            cast_done = sem("a_cast")
            wT_done, wT_copied, wp_done, wp_copied = (sem(f"a_{n}") for n in ("wT", "wTc", "wp", "wpc"))
            link_d, stats_done, var_ready, std_ready = (sem(f"a_{n}") for n in ("link", "stats", "var", "std"))
            hn_ready, t_done, hT_ready, g_done, v_done = (sem(f"a_{n}") for n in ("hn", "t", "hT", "g", "v"))
            gT_ready, vx_ready, s_done, sT_ready, sTm_ready = (sem(f"a_{n}") for n in ("gT", "vx", "s", "sT", "sTm"))
            bd_done, o_done, o_stored, state_ready, ones_ready = (
                sem(f"a_{n}") for n in ("bd", "o", "os", "state", "ones"))
            fin, xb_ready = sem("a_fin"), sem("a_xb")

            with nc.Block() as block:
                @block.sync
                def _(sp):
                    xt = x.rearrange("b (t p) c -> p (b t) c", p=P)
                    sp.dma_start(X[:], xt).then_inc(x_in, 16)
                    sp.dma_start(tab[:], consts).then_inc(const_in, 16)
                    for n, w in enumerate((a_wq, a_wk, a_wv, a_wo)):
                        sp.dma_start(aw[:, n, :], w).then_inc(aw_in, 16)
                    sp.dma_start(abo_sb[:], a_bo.partition_broadcast(P)).then_inc(aw_in, 16)
                    sp.dma_start(rw_sb[:], router_w).then_inc(bw_in, 16)
                    sp.dma_start(rb_sb[:], router_b.partition_broadcast(P)).then_inc(bw_in, 16)
                    for n, w in enumerate((b_wq, b_wk, b_wv, b_wo)):
                        sp.dma_start(bw_sb[:, n, :], w).then_inc(bw_in, 16)
                    for n, v in enumerate((b_bq, b_bk)):
                        sp.dma_start(bcol[:, n:n + 1], v.rearrange("(c o) -> c o", o=1)).then_inc(bw_in, 16)
                    for n, v in enumerate((b_bv, b_bo, b_gamma, b_beta)):
                        sp.dma_start(brow[:, n, :], v.partition_broadcast(P)).then_inc(bw_in, 16)
                    sp.dma_start(w1_sb[:], w1.rearrange("e c n -> c e n")).then_inc(w1_in, 16)
                    sp.dma_start(w2_sb[:], w2.rearrange("e (j p) c -> p e j c", p=P)).then_inc(w2_in, 16)

                @block.gpsimd
                def _(pool):
                    pool.memset(neg_ones[:], -1.0)
                    pool.memset(ones_bf[:], 1.0)
                    pool.memset(vx[:], 1.0).then_inc(ones_ready, 1)
                    pool.wait_ge(x_in, 16)
                    pool.wait_ge(cast_done, 4)
                    with pool.Fori(0, CH) as i:
                        for b in range(BATCH):
                            n = i * 2 + b + 1
                            pool.wait_ge(sT_ready, n)
                            pool.tensor_tensor(sTm[:, b, :], sT[:, b, :], keep_less_1[:], ALU.add
                                               ).then_inc(sTm_ready, 1)

                @block.vector
                def _(dve):
                    link = linker(dve, link_d)
                    dve.wait_ge(const_in, 16)
                    dve.tensor_copy(ident_bf[:], ident).then_inc(cast_done, 1)
                    dve.tensor_copy(before_bf[:], before).then_inc(cast_done, 1)
                    link(dve.tensor_tensor(keep[:], before, ident, ALU.add))
                    dve.tensor_scalar(keep_less_1[:], keep[:], 1.0, None, ALU.subtract).then_inc(cast_done, 2)
                    for b in range(BATCH):
                        dve.memset(state[:, b, :], 0.0).then_inc(state_ready, 1)
                    dve.wait_ge(x_in, 16)
                    norm_stats(dve, link, X, stats_done, var_ready, std_ready)
                    dve.wait_ge(ones_ready, 1)
                    with dve.Fori(0, CH) as i:
                        for b in range(BATCH):
                            t = i + b * CH
                            dve.tensor_scalar(hn[:, b, :], tile_of(X, t), mean[:, bass.ds(t, 1)],
                                              rstd[:, bass.ds(t, 1)], ALU.subtract, ALU.mult
                                              ).then_inc(hn_ready, 1)
                        for b in range(BATCH):
                            dve.wait_ge(v_done, i * 2 + b + 1)
                            dve.tensor_copy(vx[:, b, 0:P], banks[4 * b + 2][:, 0:P]).then_inc(vx_ready, 1)
                        for b in range(BATCH):
                            dve.wait_ge(s_done, i * 2 + b + 1)
                            dve.tensor_tensor(sT[:, b, :], banks[4 * b][:, 0:P], keep[:], ALU.mult
                                              ).then_inc(sT_ready, 1)
                        for b in range(BATCH):
                            n = i * 2 + b + 1
                            dve.wait_ge(bd_done, n)
                            dve.tensor_copy(tail[:, b, bass.ds(i, 1), :].rearrange("p a c -> p (a c)"),
                                            banks[4 * b + 3][:, 0:VX]).then_inc(fin, 1)
                        for b in range(BATCH):
                            n = i * 2 + b + 1
                            dve.wait_ge(o_done, n)
                            dve.tensor_copy(acc[:, b, bass.ds(i, 1), :].rearrange("p a c -> p (a c)"),
                                            banks[4 * b + 1][:, 0:VX]).then_inc(o_stored, 1)
                            dve.tensor_tensor(state[:, b, :], banks[4 * b + 3][:, VX:2 * VX],
                                              state[:, b, :], ALU.add).then_inc(state_ready, 1)
                    dve.wait_ge(fin, BATCH * CH)
                    dve.wait_ge(o_stored, BATCH * CH)
                    link(dve.memset(later[:, :, CH - 1, :], 0.0))
                    for c in range(CH - 2, -1, -1):
                        link(dve.tensor_tensor(later[:, :, c, :], later[:, :, c + 1, :], tail[:, :, c + 1, :],
                                               ALU.add))
                    accf = acc[:].rearrange("p b c v -> p (b c) v")
                    link(dve.tensor_tensor(accf, accf, later[:].rearrange("p b c v -> p (b c) v"), ALU.add))
                    link(dve.tensor_scalar(rden[:], accf[:, :, P], 1e-5, None, ALU.add))
                    link(dve.reciprocal(rden[:], rden[:]))
                    link(dve.tensor_tensor(work[:], accf[:, :, 0:P], rden[:].unsqueeze(2).broadcast_to([P, NT, P]),
                                           ALU.mult))
                    link(dve.tensor_tensor(work[:], work[:], abo_sb[:].unsqueeze(1).broadcast_to([P, NT, P]),
                                           ALU.add))
                    link(dve.tensor_tensor(X[:], X[:], work[:], ALU.add))

                @block.scalar
                def _(act):
                    act.wait_ge(wT_done, 1)
                    act.activation(woT[:], banks[0][:, 0:P], ACT.Copy).then_inc(wT_copied, 1)
                    act.wait_ge(wp_done, 1)
                    act.activation(gmat[:], banks[1][:, 0:P], ACT.Copy, scale=0.01).then_inc(wp_copied, 1)
                    act.activation(vmat[:], banks[1][:, P:2 * P], ACT.Copy).then_inc(wp_copied, 1)
                    norm_sqrt(act, var_ready, std_ready)
                    with act.Fori(0, CH) as i:
                        for b in range(BATCH):
                            act.wait_ge(t_done, i * 2 + b + 1)
                            act.activation(hT[:, b, :], banks[4 * b][:, 0:P], ACT.Copy).then_inc(hT_ready, 1)
                        for b in range(BATCH):
                            act.wait_ge(g_done, i * 2 + b + 1)
                            act.activation(gT[:, b, :], banks[4 * b + 1][:, 0:P], ACT.Copy).then_inc(gT_ready, 1)

                @block.tensor
                def _(pe):
                    pe.wait_ge(const_in, 16)
                    pe.wait_ge(aw_in, 16 * 5)
                    pe.transpose(banks[0][:, 0:P], aw[:, 3, :], ident).then_inc(wT_done, 1)
                    pe.matmul(banks[1][:, 0:P], aw[:, 0, :], aw[:, 1, :], start=True, stop=True)
                    pe.wait_ge(wT_copied, 1)
                    pe.matmul(banks[1][:, P:2 * P], aw[:, 2, :], woT[:], start=True, stop=True
                              ).then_inc(wp_done, 1)
                    pe.wait_ge(wp_copied, 2)
                    pe.wait_ge(ones_ready, 1)
                    with pe.Fori(0, CH) as i:
                        for b in range(BATCH):
                            pe.wait_ge(hn_ready, i * 2 + b + 1)
                            pe.transpose(banks[4 * b][:, 0:P], hn[:, b, :], ident).then_inc(t_done, 1)
                        for b in range(BATCH):
                            n = i * 2 + b + 1
                            pe.wait_ge(hT_ready, n)
                            pe.wait_ge(state_ready, n)
                            pe.matmul(banks[4 * b + 1][:, 0:P], gmat[:], hT[:, b, :], start=True, stop=True
                                      ).then_inc(g_done, 1)
                            pe.matmul(banks[4 * b + 2][:, 0:P], hT[:, b, :], vmat[:], start=True, stop=True
                                      ).then_inc(v_done, 1)
                        for b in range(BATCH):
                            pe.wait_ge(gT_ready, i * 2 + b + 1)
                            pe.matmul(banks[4 * b][:, 0:P], hT[:, b, :], gT[:, b, :], start=True, stop=True
                                      ).then_inc(s_done, 1)
                        for b in range(BATCH):
                            pe.wait_ge(vx_ready, i * 2 + b + 1)
                            pe.matmul(banks[4 * b + 3][:, 0:VX], neg_ones[:], vx[:, b, :], start=True, stop=True)
                            pe.matmul(banks[4 * b + 3][:, VX:2 * VX], hn[:, b, :], vx[:, b, :],
                                      start=True, stop=True).then_inc(bd_done, 1)
                        for b in range(BATCH):
                            pe.matmul(banks[4 * b + 1][:, 0:VX], gT[:, b, :], state[:, b, :],
                                      start=True, stop=False)
                            pe.wait_ge(sTm_ready, i * 2 + b + 1)
                            pe.matmul(banks[4 * b + 1][:, 0:VX], sTm[:, b, :], vx[:, b, :],
                                      start=False, stop=True).then_inc(o_done, 1)

        slot_i = sb("slot_i", [P, NT], I32)
        prob = sb("prob", [P, NT])

        def experts(layer, own_sb):
            tag = f"f{layer}"
            first = layer == 0

            def sb(name, shape, dt=F32):
                return own_sb(f"{tag}_{name}", shape, dt)

            hT_g = sb("hT_g", [P, 2, 4 * P])
            logit = sb("logit", [P, NT, EXPERTS])
            rt_a = sb("rt_a", [P, NT, EXPERTS])
            onehot = sb("onehot", [P, NT, EXPERTS])
            onehot_bf = sb("onehot_bf", [P, NT, EXPERTS], BF16)
            top = sb("top", [P, NT])
            slot_f = sb("slot_f", [P, NT])
            cnt = sb("cnt", [P, EXPERTS])
            cmp16 = sb("cmp16", [P, EXPERTS, NT])
            nblk = sb("nblk", [P, EXPERTS])
            cmp8 = sb("cmp8", [P, EXPERTS, EXPERTS])
            ends = sb("ends", [P, EXPERTS])
            cmpb = sb("cmpb", [1, BLOCKS, EXPERTS])
            owner_f = sb("owner_f", [1, BLOCKS])
            owner = sb("owner", [1, BLOCKS], I32)
            xin = sb("xin", [P, 2, P])
            xT = sb("xT", [P, 2, P])
            up = sb("up", [P, 2, FFN])
            gated = sb("gated", [P, 2, FFN])
            gatedT = sb("gatedT", [P, 2, FFN])
            yout = sb("yout", [P, 2, P])
            zero_pad = sb("zero_pad", [P, P])
            link_d, stats_done, var_ready, std_ready, h_ready = (
                sem(f"{tag}_{n}") for n in ("link", "stats", "var", "std", "h"))
            t_done, t_copied, l_done, e_in, e_done, oh_ready, r_done, slots_ready = (
                sem(f"{tag}_{n}") for n in ("t", "tc", "l", "ei", "e", "oh", "r", "slot"))
            zero_ready = sem(f"{tag}_zero")

            with nc.Block() as block:
                @block.vector
                def _(dve):
                    link = linker(dve, link_d)
                    norm_stats(dve, link, X, stats_done, var_ready, std_ready)
                    for t in range(NT):
                        normed(dve, H[:, t, :], X[:, t, :], t).then_inc(h_ready, 1)
                    dve.wait_ge(l_done, 1)
                    link(dve.tensor_tensor(logit[:], banks[2][:, 0:NT * EXPERTS].rearrange("p (t e) -> p t e", t=NT),
                                           rb_sb[:].unsqueeze(1).broadcast_to([P, NT, EXPERTS]), ALU.add))
                    link(dve.tensor_reduce(top[:], logit[:], AX_X, ALU.max))
                    topb = top[:].unsqueeze(2).broadcast_to([P, NT, EXPERTS])
                    revb = rank_rev.unsqueeze(1).broadcast_to([P, NT, EXPERTS])
                    dve.tensor_tensor(rt_a[:], logit[:], topb, ALU.subtract).then_inc(e_in, 1)
                    link(dve.tensor_tensor(onehot[:], logit[:], topb, ALU.is_equal))
                    link(dve.tensor_tensor(onehot[:], onehot[:], revb, ALU.mult))
                    link(dve.tensor_reduce(slot_f[:], onehot[:], AX_X, ALU.max))
                    link(dve.tensor_tensor(onehot[:], revb, slot_f[:].unsqueeze(2).broadcast_to([P, NT, EXPERTS]),
                                           ALU.is_equal))
                    dve.tensor_copy(onehot_bf[:], onehot[:]).then_inc(oh_ready, 1)
                    dve.wait_ge(e_done, 1)
                    link(dve.tensor_reduce(prob[:], rt_a[:], AX_X, ALU.add))
                    link(dve.reciprocal(prob[:], prob[:]))
                    dve.wait_ge(r_done, 1)
                    link(dve.tensor_reduce(cnt[:], banks[4][:, 0:NT * EXPERTS].rearrange("p (t e) -> p e t", t=NT),
                                           AX_X, ALU.add))
                    link(dve.tensor_tensor(cmp16[:], cnt[:].unsqueeze(2).broadcast_to([P, EXPERTS, NT]),
                                           thresholds.unsqueeze(1).broadcast_to([P, EXPERTS, NT]), ALU.is_gt))
                    link(dve.tensor_reduce(nblk[:], cmp16[:], AX_X, ALU.add))
                    link(dve.tensor_tensor(cmp8[:], nblk[:].unsqueeze(1).broadcast_to([P, EXPERTS, EXPERTS]),
                                           upto.rearrange("p (a b) -> p a b", a=EXPERTS), ALU.mult))
                    link(dve.tensor_reduce(ends[:], cmp8[:], AX_X, ALU.add))
                    link(dve.tensor_tensor(cmpb[:], ends[0:1, :].unsqueeze(1).broadcast_to([1, BLOCKS, EXPERTS]),
                                           block_no[0:1, :].unsqueeze(2).broadcast_to([1, BLOCKS, EXPERTS]),
                                           ALU.is_le))
                    link(dve.tensor_reduce(owner_f[:], cmpb[:], AX_X, ALU.add))
                    link(dve.tensor_scalar(owner[:], owner_f[:], float(EXPERTS - 1), None, ALU.min))
                    link(dve.tensor_tensor(ends[:], ends[:], nblk[:], ALU.subtract))
                    link(dve.tensor_scalar(ends[:], ends[:], float(P), None, ALU.mult))
                    link(dve.tensor_tensor(rt_a[:], banks[3][:, 0:NT * EXPERTS].rearrange("p (t e) -> p t e", t=NT),
                                           ends[:].unsqueeze(1).broadcast_to([P, NT, EXPERTS]), ALU.add))
                    link(dve.tensor_tensor(rt_a[:], rt_a[:], onehot[:], ALU.mult))
                    link(dve.tensor_reduce(slot_f[:], rt_a[:], AX_X, ALU.add))
                    dve.tensor_copy(slot_i[:], slot_f[:]).then_inc(slots_ready, 1)

                @block.scalar
                def _(act):
                    norm_sqrt(act, var_ready, std_ready)
                    for g in range(NT // 4):
                        act.wait_ge(t_done, g + 1)
                        act.activation(hT_g[:, g % 2, :], banks[g % 2][:], ACT.Copy).then_inc(t_copied, 1)
                    act.wait_ge(e_in, 1)
                    act.activation(rt_a[:], rt_a[:], ACT.Exp).then_inc(e_done, 1)

                @block.tensor
                def _(pe):
                    pe.wait_ge(bw_in, 16 * 12)

                    def logits(g):
                        pe.wait_ge(t_copied, g + 1)
                        for k in range(4):
                            t = 4 * g + k
                            last = pe.matmul(banks[2][:, t * EXPERTS:(t + 1) * EXPERTS],
                                             hT_g[:, g % 2, k * P:(k + 1) * P], rw_sb[:], start=True, stop=True)
                        if g == NT // 4 - 1:
                            last.then_inc(l_done, 1)

                    for g in range(NT // 4):
                        pe.wait_ge(h_ready, 4 * g + 4)
                        for k in range(4):
                            last = pe.transpose(banks[g % 2][:, k * P:(k + 1) * P], H[:, 4 * g + k, :], ident)
                        last.then_inc(t_done, 1)
                        if g:
                            logits(g - 1)
                    logits(NT // 4 - 1)
                    pe.wait_ge(oh_ready, 1)
                    ohf = onehot_bf[:].rearrange("p t e -> p (t e)")
                    pe.matmul(banks[4][:, 0:NT * EXPERTS], ones_bf[:], ohf, start=True, stop=True)
                    pe.matmul(banks[3][:, 0:NT * EXPERTS], before_bf[:], ohf, start=True, stop=False)
                    for t in range(NT - 1):
                        last = pe.matmul(banks[3][:, (t + 1) * EXPERTS:NT * EXPERTS], ones_bf[:],
                                         onehot_bf[:, t:t + 1, :].broadcast_to([P, NT - 1 - t, EXPERTS]),
                                         start=False, stop=(t == NT - 2))
                    last.then_inc(r_done, 1)

                @block.gpsimd
                def _(pool):
                    if first:
                        pool.memset(zero_pad[:], 0.0).then_inc(zero_ready, 1)
                        pool.wait_ge(zero_ready, 1)
                        for n in range(BLOCKS):
                            pool.dma_start(slots_dram[n * P:(n + 1) * P, :], zero_pad[:]).then_inc(pad_in, 16)
                        pool.wait_ge(pad_in, 16 * BLOCKS)
                    pool.wait_ge(slots_ready, 1)
                    pool.wait_ge(h_ready, NT)
                    for t in range(NT):
                        pool.indirect_dma_start(slots_dram, bass.IndirectOffsetOnAxis(slot_i[:, t:t + 1], 0),
                                                H[:, t, :], None).then_inc(scattered, 16)
                    pool.wait_ge(scattered, 16 * NT * (layer + 1))

            xin_ready = [sem(f"{tag}_xin{s}") for s in range(2)]
            y_out = [sem(f"{tag}_yout{s}") for s in range(2)]
            xt_done, xT_ready, up_done, up_ready, gated_ready, gt_done, gT_ready, y_done, y_ready = (
                sem(f"{tag}_{n}") for n in ("xt", "xT", "up", "upr", "gat", "gt", "gTr", "y", "yr"))

            PAIRS = (BLOCKS - 1) // 2

            def pairs(eng, body):
                body(0, True)
                with eng.Fori(1, PAIRS) as i:
                    body(i, False)

            with nc.Block() as block:
                @block.sync
                def _(sp):
                    for s in range(2):
                        sp.dma_start(xin[:, s, :], slots_dram[s * P:(s + 1) * P, :]).then_inc(xin_ready[s], 16)

                    def load(n, s):
                        sp.wait_ge(xt_done, n - 1)
                        sp.dma_start(xin[:, s, :], slots_dram[bass.ds(n * P, P), :]).then_inc(xin_ready[s], 16)

                    with sp.Fori(0, PAIRS - 1) as i:
                        for s in range(2):
                            load(i * 2 + 2 + s, s)
                    load(BLOCKS - 1, (BLOCKS - 1) % 2)

                @block.scalar
                def _(act):
                    def store(n, s):
                        act.wait_ge(y_ready, n + 1)
                        act.dma_start(ys_dram[bass.ds(n * P, P), :], yout[:, s, :]).then_inc(y_out[s], 16)

                    def silu(n, s):
                        act.wait_ge(up_done, n + 1)
                        act.activation(up[:, s, :], banks[2 * s][:], ACT.Silu).then_inc(up_ready, 1)

                    def turn(n, s):
                        act.wait_ge(gt_done, n + 1)
                        act.activation(gatedT[:, s, :], banks[4][:], ACT.Copy).then_inc(gT_ready, 1)

                    silu(0, 0)

                    def body(i, first):
                        for k in range(2):
                            turn(i * 2 + k, k)
                            silu(i * 2 + k + 1, (k + 1) % 2)
                            store(i * 2 + k, k)

                    pairs(act, body)
                    turn(BLOCKS - 1, 0)
                    store(BLOCKS - 1, 0)
                    act.wait_ge(y_out[0], 16 * (PAIRS + 1))
                    act.wait_ge(y_out[1], 16 * PAIRS)

                @block.vector
                def _(dve):
                    def enter(n, s):
                        dve.wait_ge(xt_done, n + 1)
                        dve.tensor_copy(xT[:, s, :], banks[5][:, 0:P]).then_inc(xT_ready, 1)

                    def gate(n, s):
                        dve.wait_ge(up_ready, n + 1)
                        dve.tensor_tensor(gated[:, s, :], banks[2 * s + 1][:], up[:, s, :], ALU.mult
                                          ).then_inc(gated_ready, 1)

                    def leave(n, s, stored, first=False):
                        dve.wait_ge(y_done, n + 1)
                        if not first:
                            dve.wait_ge(y_out[s], 16 * stored)
                        dve.tensor_copy(yout[:, s, :], banks[6][:, 0:P]).then_inc(y_ready, 1)

                    enter(0, 0)

                    def body(i, first):
                        for k in range(2):
                            enter(i * 2 + k + 1, (k + 1) % 2)
                            gate(i * 2 + k, k)
                            leave(i * 2 + k, k, i, first)

                    pairs(dve, body)
                    gate(BLOCKS - 1, 0)
                    leave(BLOCKS - 1, 0, PAIRS)

                @block.tensor
                def _(pe):
                    pe.wait_ge(w1_in, 16)
                    pe.wait_ge(w2_in, 16)

                    def expert_of(n):
                        return pe.value_load(owner[0:1, bass.ds(n, 1)], min_val=0, max_val=EXPERTS - 1)

                    def enter(n, s, use):
                        pe.wait_ge(xin_ready[s], 16 * use)
                        pe.transpose(banks[5][:, 0:P], xin[:, s, :], ident).then_inc(xt_done, 1)

                    def turn(n, s):
                        pe.wait_ge(gated_ready, n + 1)
                        for j in range(FJ):
                            last = pe.transpose(banks[4][:, j * P:(j + 1) * P], gated[:, s, j * P:(j + 1) * P],
                                                ident)
                        last.then_inc(gt_done, 1)

                    def up_product(n, s):
                        e = expert_of(n)
                        pe.wait_ge(xT_ready, n + 1)
                        for half in range(2):
                            last = pe.matmul(banks[2 * s + half][:], xT[:, s, :],
                                             w1_sb[:, bass.ds(e, 1), half * FFN:(half + 1) * FFN]
                                             .rearrange("p a n -> p (a n)"), start=True, stop=True)
                        last.then_inc(up_done, 1)

                    def down_product(n, s, first=False):
                        e = expert_of(n)
                        pe.wait_ge(gT_ready, n + 1)
                        if not first:
                            pe.wait_ge(y_ready, n)
                        for j in range(FJ):
                            last = pe.matmul(banks[6][:, 0:P], gatedT[:, s, j * P:(j + 1) * P],
                                             w2_sb[:, bass.ds(e, 1), j, :].rearrange("p a n -> p (a n)"),
                                             start=(j == 0), stop=(j == FJ - 1))
                        last.then_inc(y_done, 1)

                    enter(0, 0, 1)
                    up_product(0, 0)

                    def body(i, first):
                        for k in range(2):
                            n = i * 2 + k
                            enter(n + 1, (k + 1) % 2, i + 1 + k)
                            turn(n, k)
                            up_product(n + 1, (k + 1) % 2)
                            down_product(n, k, first and k == 0)

                    pairs(pe, body)
                    turn(BLOCKS - 1, 0)
                    down_product(BLOCKS - 1, 0)

            with nc.Block() as block:
                @block.gpsimd
                def _(pool):
                    for t in range(NT):
                        pool.indirect_dma_start(work[:, t, :], None, ys_dram,
                                                bass.IndirectOffsetOnAxis(slot_i[:, t:t + 1], 0)
                                                ).then_inc(gathered[t // 4], 16)

                @block.vector
                def _(dve):
                    for g in range(4):
                        dve.wait_ge(gathered[g], 16 * 4 * (layer + 1))
                        for t in range(4 * g, 4 * g + 4):
                            dve.scalar_tensor_tensor(X[:, t, :], work[:, t, :], prob[:, t:t + 1], X[:, t, :],
                                                     ALU.mult, ALU.add).then_inc(x_done, 1)

            return None

        def softmax_attention(stack):
            sb = own(stack)
            ctxb = sb("ctxb", [P, NT, P])
            vall = sb("vall", [P, BATCH, KT, P])
            hT_g = sb("b_hT", [P, 2, 4 * P])

            def project(sb):
                full = sb("full", [P, 2, 2, QH])
                rest = sb("rest", [P, 2, 2, QH])
                parts = sb("parts", [P, 2, 2, PARTS, QH], BF16)
                zero_one = sb("zero_one", [P, 2, SEQ], BF16)
                link_d, stats_done, var_ready, std_ready, h_ready = (
                    sem(f"b_{n}") for n in ("link", "stats", "var", "std", "h"))
                t_done, t_copied, qk_done, v_done, head_ready, rest_ready, mid_ready, low_ready, v_ready = (
                    sem(f"b_{n}") for n in ("t", "tc", "qk", "v", "hd", "rs", "md", "lw", "vr"))
                rows_ready, rows_out = sem("b_rows"), sem("b_rows_out")
                parts_out = [[sem(f"b_out{o}{s}") for s in range(2)] for o in range(2)]
                NG = NT // 4

                with nc.Block() as block:
                    @block.gpsimd
                    def _(pool):
                        pool.memset(zero_one[:, 0, :], 0.0).then_inc(rows_ready, 1)
                        pool.memset(zero_one[:, 1, :], 1.0).then_inc(rows_ready, 1)

                    @block.vector
                    def _(dve):
                        link = linker(dve, link_d)
                        norm_stats(dve, link, X, stats_done, var_ready, std_ready)
                        for t in range(NT):
                            normed(dve, H[:, t, :], X[:, t, :], t).then_inc(h_ready, 1)

                        def split(n):
                            g, o = n // 2, n % 2
                            dve.wait_ge(head_ready, n + 1)
                            dve.tensor_tensor(rest[:, o, g % 2, :], full[:, o, g % 2, :],
                                              parts[:, o, g % 2, 0, :], ALU.subtract).then_inc(rest_ready, 1)

                        def low(n):
                            g, o = n // 2, n % 2
                            dve.wait_ge(mid_ready, n + 1)
                            dve.tensor_tensor(parts[:, o, g % 2, 2, :], rest[:, o, g % 2, :],
                                              parts[:, o, g % 2, 1, :], ALU.subtract).then_inc(low_ready, 1)

                        for n in range(2 * NG):
                            g = n // 2
                            split(n)
                            if n:
                                low(n - 1)
                            if n % 2:
                                dve.wait_ge(v_done, g + 1)
                                dve.tensor_tensor(vall[:, g // 2, g % 2 * 4:g % 2 * 4 + 4, :],
                                                  banks[4 + 3 * (g % 2)].rearrange("p (t c) -> p t c", t=4),
                                                  brow[:, 0:1, :].broadcast_to([P, 4, P]), ALU.add
                                                  ).then_inc(v_ready, 1)
                        low(2 * NG - 1)

                    @block.scalar
                    def _(act):
                        norm_sqrt(act, var_ready, std_ready)

                        def turned(g):
                            act.wait_ge(t_done, g + 1)
                            act.activation(hT_g[:, g % 2, :], banks[g % 2], ACT.Copy).then_inc(t_copied, 1)

                        def head(n):
                            g, o = n // 2, n % 2
                            act.wait_ge(qk_done, n + 1)
                            if g >= 2:
                                act.wait_ge(parts_out[o][g % 2], 16 * len(PRODUCTS) * (g // 2))
                                act.wait_ge(low_ready, n - 3)
                            src = banks[2 + o + 3 * (g % 2)]
                            act.activation(full[:, o, g % 2, :], src, ACT.Identity, bias=bcol[:, o:o + 1])
                            act.activation(parts[:, o, g % 2, 0, :], src, ACT.Identity,
                                           bias=bcol[:, o:o + 1]).then_inc(head_ready, 1)

                        def middle(n):
                            g, o = n // 2, n % 2
                            act.wait_ge(rest_ready, n + 1)
                            act.activation(parts[:, o, g % 2, 1, :], rest[:, o, g % 2, :], ACT.Copy
                                           ).then_inc(mid_ready, 1)

                        turned(0)
                        for n in range(2 * NG):
                            if n % 2 and n // 2 + 1 < NG:
                                turned(n // 2 + 1)
                            head(n)
                            if n:
                                middle(n - 1)
                        middle(2 * NG - 1)

                    @block.tensor
                    def _(pe):
                        def turn(g):
                            pe.wait_ge(h_ready, 4 * g + 4)
                            for k in range(4):
                                last = pe.transpose(banks[g % 2][:, k * P:(k + 1) * P], H[:, 4 * g + k, :], ident)
                            last.then_inc(t_done, 1)

                        turn(0)
                        for g in range(NG):
                            if g + 1 < NG:
                                turn(g + 1)
                            pe.wait_ge(t_copied, g + 1)
                            base = 2 + 3 * (g % 2)
                            for o in range(2):
                                if g >= 2:
                                    pe.wait_ge(head_ready, 2 * (g - 2) + o + 1)
                                pe.matmul(banks[base + o], bw_sb[:, o, :], hT_g[:, g % 2, :], start=True, stop=True
                                          ).then_inc(qk_done, 1)
                            if g >= 2:
                                pe.wait_ge(v_ready, g - 1)
                            for k in range(4):
                                last = pe.matmul(banks[base + 2][:, k * P:(k + 1) * P],
                                                 hT_g[:, g % 2, k * P:(k + 1) * P], bw_sb[:, 2, :],
                                                 start=True, stop=True)
                            last.then_inc(v_done, 1)

                    @block.sync
                    def _(sp):
                        sp.wait_ge(rows_ready, 2)
                        for n, stack_ in enumerate((qd, kd)):
                            sp.dma_start(stack_[:, SHIFT_ROW:SHIFT_ROW + PARTS, :],
                                         zero_one[0:BATCH * HEADS * PARTS, n, :]).then_inc(rows_out, 16)
                        for n in range(2 * NG):
                            g, o = n // 2, n % 2
                            sp.wait_ge(low_ready, n + 1)
                            b, t0 = g // 2, g % 2 * QH
                            for m, pair in enumerate(PRODUCTS):
                                dst = (qd, kd)[o][b * HEADS:(b + 1) * HEADS, PROW[m]:PROW[m] + DK, t0:t0 + QH]
                                sp.dma_start(dst, parts[:, o, g % 2, pair[o], :]).then_inc(parts_out[o][g % 2], 16)
                        sp.wait_ge(rows_out, 32)
                        for o in range(2):
                            for s in range(2):
                                sp.wait_ge(parts_out[o][s], 16 * len(PRODUCTS) * (NG // 2))

            def attend(sb):
                qst = sb("qst", [P, UNITS, 2, QH], BF16)
                kst = sb("kst", [P, BATCH, 2, SEQ], BF16)
                vst = sb("vst", [P, BATCH, KT, HG, 32])
                probs = sb("probs", [P, 4, HG, QH])
                mx = sb("mx", [P, QT, 2, HG])
                shift = sb("shift", [P, QT, HG])
                shift_rest = sb("shift_rest", [P, QT, HG])
                shift_parts = sb("shift_parts", [P, QT, HG, PARTS], BF16)
                shift_rows = sb("shift_rows", [HG * PARTS, 2, QH], BF16)
                ctxT = sb("ctxT", [P, QH])
                rden = sb("b_rden", [P, QT, HG])
                q_in = [sem(f"q_in{s}") for s in range(UNITS)]
                k_in = [sem(f"k_in{b}") for b in range(BATCH)]
                shift_in = [sem(f"shift_in{s}") for s in range(UNITS)]
                v_staged = [sem(f"v_staged{b}") for b in range(BATCH)]
                score_done = [sem(f"score{p}") for p in range(2)]
                exp_done = [sem(f"exp{p}") for p in range(2)]
                max_scores = [sem(f"msc{p}") for p in range(2)]
                max_read = [sem(f"mrd{p}") for p in range(2)]
                pv_done = [sem(f"pv{s}") for s in range(4)]
                shift_link, parts_ready, rows_done, rows_ready = (
                    sem(f"sh_{n}") for n in ("link", "parts", "done", "rows"))
                ctxT_ready, ctx_turned, rden_ready, ctx_ready, v_clear = (
                    sem(f"cx_{n}") for n in ("T", "turn", "rden", "ready", "vclear"))
                qsrc = qd.rearrange("(g pair r) row t -> g r row pair t", pair=2, r=2)
                ksrc = kd.rearrange("(g pair r) row t -> g r row pair t", pair=2, r=2)
                TOP = 8 * UNITS


                def rounds(eng, body):
                    body(0, True, False)
                    with eng.Fori(1, HGROUPS - 1) as i:
                        body(i, False, False)
                    body(HGROUPS - 1, False, True)

                with nc.Block() as block:
                    @block.sync
                    def _(sp):
                        def load_q(i, s):
                            b, half = s // 2, s % 2
                            for r in range(2):
                                src = qsrc[bass.ds(i + b * HGROUPS, 1), r, :, :, half * QH:(half + 1) * QH]
                                sp.dma_start(qst[64 * r:64 * r + ROWS, s, :, :],
                                             src.rearrange("g row pair t -> (g row) pair t")).then_inc(q_in[s], 16)

                        def load_k(i, b):
                            for r in range(2):
                                src = ksrc[bass.ds(i + b * HGROUPS, 1), r, :, :, :]
                                sp.dma_start(kst[64 * r:64 * r + ROWS, b, :, :],
                                             src.rearrange("g row pair t -> (g row) pair t")).then_inc(k_in[b], 16)

                        def load_shift(u, s):
                            sp.wait_ge(rows_ready, u + 1)
                            for j in range(HG):
                                row = 64 * (j % 2) + SHIFT_ROW
                                sp.dma_start(qst[row:row + PARTS, s, j // 2, :],
                                             shift_rows[j * PARTS:(j + 1) * PARTS, s % 2, :]
                                             ).then_inc(shift_in[s], 16)

                        def body(i, first, last):
                            for s in range(UNITS):
                                u = i * UNITS + s
                                if not (last and s == UNITS - 1):
                                    load_shift(u + 1, (s + 1) % UNITS)
                                if not last:
                                    sp.wait_ge(score_done[1], u * KT + KT)
                                    load_q(i + 1, s)
                                    if s % 2:
                                        load_k(i + 1, s // 2)

                        load_k(0, 0)
                        load_q(0, 0)
                        load_q(0, 1)
                        load_k(0, 1)
                        load_q(0, 2)
                        load_q(0, 3)
                        load_shift(0, 0)
                        rounds(sp, body)

                    @block.gpsimd
                    def _(pool):
                        pool.memset(vst[:], 0.0).then_inc(v_clear, 1)
                        pool.wait_ge(v_clear, 1)
                        pool.memset(vst[:, :, :, :, DK:DK + 1], 1.0).then_inc(v_clear, 1)

                        def stage(i, b):
                            pool.tensor_copy(vst[:, b, :, :, 0:DK],
                                             vall[:, b, :, bass.ds(i * HG * DK, HG * DK)]
                                             .rearrange("p t (h d) -> p t h d", h=HG)).then_inc(v_staged[b], 1)

                        for b in range(BATCH):
                            stage(0, b)
                        with pool.Fori(1, HGROUPS) as i:
                            for b in range(BATCH):
                                pool.wait_ge(pv_done[3], (i - 1) * 2 * UNITS + 4 * b + 4)
                                stage(i, b)
                        pool.tensor_tensor(H[:], H[:], brow[:, 1:2, :].broadcast_to([P, NT, P]), ALU.add)

                    @block.vector
                    def _(dve):
                        def maxima(u, s, n0, n1):
                            for n in range(n0, n1):
                                dve.wait_ge(max_scores[n % 2], u * 16 + n // 2 + 1)
                                dve.tensor_reduce(mx[:, n // 8, n // 4 % 2, n % 4:n % 4 + 1], banks[4 + n % 2],
                                                  AX_X, ALU.max).then_inc(max_read[n % 2], 1)

                        def make_shift(u):
                            dve.wait_ge(max_read[0], u * 16 + 16)
                            dve.wait_ge(max_read[1], u * 16 + 16)
                            dve.tensor_reduce(shift[:], mx[:].rearrange("p q k h -> p q h k"), AX_X, ALU.max,
                                              negate=True).then_inc(shift_link, 1)
                            dve.wait_ge(shift_link, u * 4 + 1)
                            dve.tensor_copy(shift_parts[:, :, :, 0], shift[:]).then_inc(shift_link, 1)
                            dve.wait_ge(shift_link, u * 4 + 2)
                            dve.tensor_tensor(shift_rest[:], shift[:], shift_parts[:, :, :, 0], ALU.subtract
                                              ).then_inc(shift_link, 1)
                            dve.wait_ge(shift_link, u * 4 + 3)
                            dve.tensor_copy(shift_parts[:, :, :, 1], shift_rest[:]).then_inc(shift_link, 1)
                            dve.wait_ge(shift_link, u * 4 + 4)
                            dve.tensor_tensor(shift_parts[:, :, :, 2], shift_rest[:], shift_parts[:, :, :, 1],
                                              ALU.subtract).then_inc(parts_ready, 1)

                        def normalise(i, s):
                            u = i * UNITS + s
                            dve.wait_ge(ctx_turned, u + 1)
                            turned = banks[7].rearrange("p (q h d) -> p q h d", q=QT, h=HG)
                            dve.reciprocal(rden[:], turned[:, :, :, DK]).then_inc(rden_ready, 1)
                            dve.wait_ge(rden_ready, u + 1)
                            dve.tensor_tensor(ctxb[:, QT * s:QT * (s + 1), bass.ds(i * HG * DK, HG * DK)]
                                              .rearrange("p q (h d) -> p q h d", h=HG),
                                              turned[:, :, :, 0:DK],
                                              rden[:].unsqueeze(3).broadcast_to([P, QT, HG, DK]), ALU.mult
                                              ).then_inc(ctx_ready, 1)

                        def body(i, first, last):
                            for s in range(UNITS):
                                u = i * UNITS + s
                                for kt in range(KT):
                                    if kt < 4 and not (last and s == UNITS - 1):
                                        maxima(u + 1, s + 1, 16 + 4 * kt, 20 + 4 * kt)
                                    if kt == 2 and not (first and s == 0):
                                        normalise(i if s else i - 1, (s - 1) % UNITS)
                                    if kt == 3 and not (last and s == UNITS - 1):
                                        make_shift(u + 1)
                                    if kt >= 4 and not (last and s >= UNITS - 2):
                                        maxima(u + 2, s + 2, 4 * kt - 16, 4 * kt - 12)

                        maxima(0, 0, 0, 32)
                        make_shift(0)
                        maxima(1, 1, 0, 16)
                        rounds(dve, body)
                        normalise(HGROUPS - 1, UNITS - 1)

                    @block.scalar
                    def _(act):
                        def copy_ctx(u):
                            act.wait_ge(pv_done[3], u * 2 + 2)
                            act.activation(ctxT[:], banks[6], ACT.Copy).then_inc(ctxT_ready, 1)

                        def copy_rows(u, s):
                            act.wait_ge(rows_done, u + 1)
                            act.activation(shift_rows[:, s % 2, :], banks[7][0:HG * PARTS, :].bitcast(BF16)[:, 0:QH],
                                           ACT.Copy).then_inc(rows_ready, 1)

                        def body(i, first, last):
                            for s in range(UNITS):
                                u = i * UNITS + s
                                for kt in range(KT):
                                    for pair in range(2):
                                        act.wait_ge(score_done[pair], u * KT + kt + 1)
                                        if pair == 0 and not (first and s == 0 and kt < 4):
                                            act.wait_ge(pv_done[kt % 4], u * 2 + kt // 4)
                                        act.activation(probs[:, kt % 4, 2 * pair:2 * pair + 2, :],
                                                       psum[:, 2 * pair:2 * pair + 2, :], ACT.Exp, scale=SCALE
                                                       ).then_inc(exp_done[pair], 1)
                                    if kt == 0 and not (first and s == 0):
                                        copy_ctx(u - 1)
                                    if kt == 5 and not (last and s == UNITS - 1):
                                        copy_rows(u + 1, s + 1)

                        copy_rows(0, 0)
                        rounds(act, body)
                        copy_ctx(HGROUPS * UNITS - 1)

                    @block.tensor
                    def _(pe):
                        def scores_for_max(i, s, u, n0, n1):
                            b = s // 2
                            if n0 == 0:
                                pe.wait_ge(q_in[s], (i + 1) * 32)
                                pe.wait_ge(k_in[b], (i + 1) * 32)
                            for n in range(n0, n1):
                                qt, kh, j = n // 8, n // 4 % 2, n % 4
                                base = 64 * (j % 2)
                                if not (isinstance(u, int) and u == 0 and n < 2):
                                    pe.wait_ge(max_read[n % 2], u * 16 + n // 2)
                                pe.matmul(banks[4 + n % 2], qst[base:base + ROWS, s, j // 2, qt * P:(qt + 1) * P],
                                          kst[base:base + ROWS, b, j // 2, kh * 512:(kh + 1) * 512],
                                          start=True, stop=True).then_inc(max_scores[n % 2], 1)

                        def shift_to_rows(u):
                            pe.wait_ge(parts_ready, u + 1)
                            for qt in range(QT):
                                last = pe.transpose(banks[7][0:HG * PARTS, :].bitcast(BF16)[:, qt * P:(qt + 1) * P],
                                                    shift_parts[:, qt, :, :].rearrange("p h n -> p (h n)"),
                                                    ident_bf[:])
                            last.then_inc(rows_done, 1)

                        def scores(u, s, kt, first):
                            for pair in range(2):
                                if not (first and s == 0 and kt == 0):
                                    pe.wait_ge(exp_done[pair], u * KT + kt)
                                for r in range(2):
                                    last = pe.matmul(banks[2 * pair + r],
                                                     kst[64 * r:64 * r + ROWS, s // 2, pair, kt * P:(kt + 1) * P],
                                                     qst[64 * r:64 * r + ROWS, s, pair, :], start=True, stop=True)
                                last.then_inc(score_done[pair], 1)

                        def weigh_values(i, u, s, kt):
                            pe.wait_ge(exp_done[0], u * KT + kt + 1)
                            pe.wait_ge(exp_done[1], u * KT + kt + 1)
                            if kt == 0:
                                pe.wait_ge(v_staged[s // 2], i + 1)
                                if not (isinstance(u, int) and u == 0):
                                    pe.wait_ge(ctxT_ready, u)
                            for j in range(HG):
                                last = pe.matmul(banks[6][32 * j:32 * (j + 1), :], vst[:, s // 2, kt, j, :],
                                                 probs[:, kt % 4, j, :], start=(kt == 0), stop=(kt == KT - 1))
                            last.then_inc(pv_done[kt % 4], 1)

                        def turn_ctx(u):
                            pe.wait_ge(ctxT_ready, u + 1)
                            for qt in range(QT):
                                last = pe.transpose(banks[7][:, qt * P:(qt + 1) * P], ctxT[:, qt * P:(qt + 1) * P],
                                                    ident)
                            last.then_inc(ctx_turned, 1)

                        def body(i, first, last):
                            for s in range(UNITS):
                                u = i * UNITS + s
                                before_it = not (first and s == 0)
                                for kt in range(KT):
                                    if kt == 0:
                                        pe.wait_ge(shift_in[s], (i + 1) * 16 * HG)
                                    scores(u, s, kt, first)
                                    if kt < 4 and not (last and s == UNITS - 1):
                                        scores_for_max(i + (s + 1) // UNITS, (s + 1) % UNITS, u + 1,
                                                       16 + 4 * kt, 20 + 4 * kt)
                                    if kt >= 4 and not (last and s >= UNITS - 2):
                                        scores_for_max(i + (s + 2) // UNITS, (s + 2) % UNITS, u + 2,
                                                       4 * kt - 16, 4 * kt - 12)
                                    if kt:
                                        weigh_values(i, u, s, kt - 1)
                                    elif before_it:
                                        weigh_values(i if s else i - 1, u - 1, (s - 1) % UNITS, KT - 1)
                                    if kt == 2 and before_it:
                                        turn_ctx(u - 1)
                                    if kt == 5 and not (last and s == UNITS - 1):
                                        if before_it:
                                            pe.wait_ge(ctx_ready, u)
                                        shift_to_rows(u + 1)

                        pe.wait_ge(v_clear, 2)
                        scores_for_max(0, 0, 0, 0, 32)
                        scores_for_max(0, 1, 1, 0, 16)
                        shift_to_rows(0)
                        rounds(pe, body)
                        weigh_values(HGROUPS - 1, HGROUPS * UNITS - 1, UNITS - 1, KT - 1)
                        pe.wait_ge(ctx_ready, HGROUPS * UNITS - 1)
                        turn_ctx(HGROUPS * UNITS - 1)

            def output():
                link_d, stats_done, var_ready, std_ready = (sem(f"o_{n}") for n in ("link", "stats", "var", "std"))
                t_done, t_copied, p_done, y_ready, n_ready = (sem(f"o_{n}") for n in ("t", "tc", "p", "y", "n"))
                NG = NT // 4
                with nc.Block() as block:
                    @block.vector
                    def _(dve):
                        link = linker(dve, link_d)
                        for g in range(NG):
                            dve.wait_ge(p_done, g + 1)
                            dve.tensor_tensor(work[:, 4 * g:4 * g + 4, :],
                                              banks[2 + g % 2].rearrange("p (t c) -> p t c", t=4),
                                              H[:, 4 * g:4 * g + 4, :], ALU.add).then_inc(y_ready, 1)
                        dve.wait_ge(y_ready, NG)
                        norm_stats(dve, link, work, stats_done, var_ready, std_ready)
                        for t in range(NT):
                            normed(dve, H[:, t, :], work[:, t, :], t).then_inc(n_ready, 1)
                        dve.wait_ge(n_ready, NT)
                        link(dve.tensor_tensor(H[:], H[:], brow[:, 2:3, :].broadcast_to([P, NT, P]), ALU.mult))
                        link(dve.tensor_tensor(H[:], H[:], brow[:, 3:4, :].broadcast_to([P, NT, P]), ALU.add))
                        link(dve.tensor_tensor(X[:], X[:], H[:], ALU.add))

                    @block.scalar
                    def _(act):
                        for g in range(NG):
                            act.wait_ge(t_done, g + 1)
                            act.activation(hT_g[:, g % 2, :], banks[g % 2], ACT.Copy).then_inc(t_copied, 1)
                        norm_sqrt(act, var_ready, std_ready)

                    @block.tensor
                    def _(pe):
                        def turn(g):
                            for k in range(4):
                                last = pe.transpose(banks[g % 2][:, k * P:(k + 1) * P], ctxb[:, 4 * g + k, :], ident)
                            last.then_inc(t_done, 1)

                        turn(0)
                        for g in range(NG):
                            if g + 1 < NG:
                                turn(g + 1)
                            pe.wait_ge(t_copied, g + 1)
                            if g >= 2:
                                pe.wait_ge(y_ready, g - 1)
                            for k in range(4):
                                last = pe.matmul(banks[2 + g % 2][:, k * P:(k + 1) * P],
                                                 hT_g[:, g % 2, k * P:(k + 1) * P], bw_sb[:, 3, :],
                                                 start=True, stop=True)
                            last.then_inc(p_done, 1)

            with ExitStack() as inner:
                project(own(inner))
            with ExitStack() as inner:
                attend(own(inner))
            output()

        x_done = sem("x_done")
        used.clear()
        with ExitStack() as semaphores:
            scope.append(semaphores)
            with ExitStack() as stack:
                linear_attention(own(stack))
            with ExitStack() as stack:
                experts(0, own(stack))
            with nc.Block() as block:
                @block.sync
                def _(sp):
                    for s in used:
                        sp.sem_clear(s)
            scope.pop()
        with ExitStack() as stack:
            softmax_attention(stack)
        with ExitStack() as stack:
            experts(1, own(stack))
        final = sem("final")
        with nc.Block() as block:
            @block.sync
            def _(sp):
                sp.dma_start(out.rearrange("b (t p) c -> p (b t) c", p=P), X[:]).then_inc(final, 16)
                sp.wait_ge(final, 16)


_INS = ["L0_attn_a_x", "L0_attn_a_Wq", "L0_attn_a_Wk", "L0_attn_a_Wv", "L0_attn_a_Wo", "L0_attn_a_bo",
        "L0_attn_b_Wq", "L0_attn_b_bq", "L0_attn_b_Wk", "L0_attn_b_bk", "L0_attn_b_Wv", "L0_attn_b_bv",
        "L0_attn_b_Wo", "L0_attn_b_bo", "L0_attn_b_gamma", "L0_attn_b_beta", "L0_ffn_router_w",
        "L0_ffn_router_b", "L0_ffn_w1", "L0_ffn_w2"]


def kernel(**inputs):
    import numpy as np
    import concourse.bacc as bacc
    from concourse.bass_utils import run_bass_kernel_spmd

    nc = bacc.Bacc("TRN2", target_bir_lowering=False, num_devices=1)
    arrays = {name: np.ascontiguousarray(inputs[name]) for name in _INS}
    arrays["shape_tables"] = constants()
    args = [nc.dram_tensor(name, a.shape, mybir.dt.from_np(a.dtype), kind="ExternalInput").ap()
            for name, a in arrays.items()]
    out = nc.dram_tensor("out", inputs["L0_attn_a_x"].shape, F32, kind="ExternalOutput").ap()
    hybrid_layer(nc, *args, out)
    r = run_bass_kernel_spmd(nc, [arrays], core_ids=[0])
    return r.results[0]["out"]
```

```python
from contextlib import ExitStack

import concourse.bass as bass
from concourse import mybir

F32 = mybir.dt.float32
BF16 = mybir.dt.bfloat16
I32 = mybir.dt.int32
ACT = mybir.ActivationFunctionType
ALU = mybir.AluOpType
AX_X = mybir.AxisListType.X

P = 128
BATCH, SEQ = 2, 1024
NT = BATCH * SEQ // P
CH = SEQ // P
LN_EPS = 1e-5
EXPERTS, FFN = 8, 512
FJ = FFN // P
BLOCKS = NT + EXPERTS - 1
HEADS, DK = 16, 8
HG = 4
QH = 512
PARTS = 3
PRODUCTS = [(0, 0), (0, 1), (1, 0), (0, 2), (1, 1), (2, 0)]
SHIFT_ROW = 4 * DK
ROWS = len(PRODUCTS) * DK + PARTS
PROW = [n * DK if n < 4 else n * DK + PARTS for n in range(len(PRODUCTS))]
SCALE = (1.0 / DK) ** 0.5
HGROUPS = HEADS // HG
UNITS = BATCH * SEQ // QH
KT = SEQ // P
QT = QH // P


def constants():
    import numpy as np
    p = np.arange(P)
    e = np.arange(EXPERTS)
    rows = [
        np.eye(P),
        (p[:, None] < p[None, :]),
        np.tile(EXPERTS - e, (P, 1)),
        np.tile(P * np.arange(NT), (P, 1)),
        np.tile((e[None, :] <= e[:, None]).reshape(1, -1), (P, 1)),
        np.tile(np.arange(BLOCKS), (P, 1)),
    ]
    return np.ascontiguousarray(np.concatenate(rows, axis=1).astype(np.float32))


CONST_COLS = 2 * P + EXPERTS + NT + EXPERTS * EXPERTS + BLOCKS


def hybrid_layer(nc, x, a_wq, a_wk, a_wv, a_wo, a_bo, b_wq, b_bq, b_wk, b_bk, b_wv, b_bv, b_wo, b_bo,
                 b_gamma, b_beta, router_w, router_b, w1, w2, consts, out):
    with ExitStack() as ctx:
        def sb(name, shape, dt=F32):
            return ctx.enter_context(nc.sbuf_tensor(name, shape, dt))

        scope = [ctx]
        used = []

        def sem(name):
            used.append(scope[-1].enter_context(nc.semaphore(name)))
            return used[-1]

        def own(stack):
            return lambda name, shape, dt=F32: stack.enter_context(nc.sbuf_tensor(name, shape, dt))

        def dram(name, shape, dt):
            return nc.dram_tensor(name, shape, dt, kind="Internal").ap()

        psum = ctx.enter_context(nc.psum_tensor("psum", [P, 8, 512], F32))
        banks = [psum[:, n, :] for n in range(8)]

        X = sb("X", [P, NT, P])
        H = sb("H", [P, NT, P])
        work = sb("work", [P, NT, P])
        tab = sb("tab", [P, CONST_COLS])
        ident = tab[:, 0:P]
        before = tab[:, P:2 * P]
        at = 2 * P
        rank_rev = tab[:, at:at + EXPERTS]
        at += EXPERTS
        thresholds = tab[:, at:at + NT]
        at += NT
        upto = tab[:, at:at + EXPERTS * EXPERTS]
        at += EXPERTS * EXPERTS
        block_no = tab[:, at:at + BLOCKS]
        ident_bf = sb("ident_bf", [P, P], BF16)
        before_bf = sb("before_bf", [P, P], BF16)
        ones_bf = sb("ones_bf", [P, P], BF16)
        neg_ones = sb("neg_ones", [P, P])
        zero_pad = sb("zero_pad", [P, P])
        w1_sb = sb("w1_sb", [P, EXPERTS, 2 * FFN])
        w2_sb = sb("w2_sb", [P, EXPERTS, FJ, P])
        rw_sb = sb("rw_sb", [P, EXPERTS])
        rb_sb = sb("rb_sb", [P, EXPERTS])
        abo_sb = sb("abo_sb", [P, P])
        bw_sb = sb("bw_sb", [P, 4, P])
        bcol = sb("bcol", [P, 2])
        brow = sb("brow", [P, 4, P])
        stats = sb("stats", [P, NT, 6])
        mean = sb("mean", [P, NT])
        var = sb("var", [P, NT])
        rstd = sb("rstd", [P, NT])
        ln_a = sb("ln_a", [P, NT])
        ln_b = sb("ln_b", [P, NT])
        const_in = sem("const_in")
        w1_in, w2_in, bw_in = sem("w1_in"), sem("w2_in"), sem("bw_in")
        pad_in = sem("pad_in")
        scattered = sem("scattered")
        gathered = [sem(f"gathered{g}") for g in range(4)]

        slots_dram = dram("slots", [BLOCKS * P, P], F32)
        ys_dram = dram("ys", [BLOCKS * P, P], F32)
        qd = dram("q_stack", [BATCH * HEADS, ROWS, SEQ], BF16)
        kd = dram("k_stack", [BATCH * HEADS, ROWS, SEQ], BF16)

        def tile_of(t, i):
            return t[:, bass.ds(i, 1), :].rearrange("p a b -> p (a b)")

        def linker(eng, done):
            count = [0]

            def link(ins):
                count[0] += 1
                ins.then_inc(done, 1)
                eng.wait_ge(done, count[0])
            return link

        def norm_stats(dve, link, src, stats_done, var_ready, std_ready):
            with dve.Fori(0, NT // 4) as i:
                for k in range(4):
                    dve.bn_stats(stats[:, bass.ds(i * 4 + k, 1), :].rearrange("p a b -> p (a b)"),
                                 tile_of(src, i * 4 + k)).then_inc(stats_done, 1)
            dve.wait_ge(stats_done, NT)
            link(dve.tensor_tensor(mean[:], stats[:, :, 1], stats[:, :, 4], ALU.add))
            link(dve.tensor_scalar(mean[:], mean[:], 0.5, None, ALU.mult))
            link(dve.tensor_tensor(ln_a[:], stats[:, :, 1], stats[:, :, 4], ALU.subtract))
            link(dve.scalar_tensor_tensor(ln_a[:], ln_a[:], 0.25, ln_a[:], ALU.mult, ALU.mult))
            link(dve.tensor_tensor(ln_b[:], stats[:, :, 2], stats[:, :, 5], ALU.add))
            link(dve.scalar_tensor_tensor(var[:], ln_b[:], 1.0 / P, ln_a[:], ALU.mult, ALU.add))
            dve.tensor_scalar(var[:], var[:], LN_EPS, None, ALU.add).then_inc(var_ready, 1)
            dve.wait_ge(std_ready, 1)
            link(dve.reciprocal(rstd[:], ln_a[:]))
            link(dve.tensor_tensor(ln_b[:], rstd[:], rstd[:], ALU.mult))
            link(dve.tensor_tensor(ln_b[:], ln_b[:], var[:], ALU.mult))
            link(dve.tensor_scalar(ln_b[:], ln_b[:], -0.5, 1.5, ALU.mult, ALU.add))
            link(dve.tensor_tensor(rstd[:], rstd[:], ln_b[:], ALU.mult))

        def norm_sqrt(act, var_ready, std_ready):
            act.wait_ge(var_ready, 1)
            act.activation(ln_a[:], var[:], ACT.Sqrt).then_inc(std_ready, 1)

        def normed(dve, dst, src, t):
            return dve.tensor_scalar(dst, src, mean[:, t:t + 1], rstd[:, t:t + 1], ALU.subtract, ALU.mult)

        def linear_attention(sb):
            VX = P + 1
            aw = sb("aw", [P, 4, P])
            woT = sb("woT", [P, P])
            gmat = sb("gmat", [P, P])
            vmat = sb("vmat", [P, P])
            hn = sb("hn", [P, BATCH, P])
            hT = sb("hT_a", [P, BATCH, P])
            gT = sb("gT", [P, BATCH, P])
            vx = sb("vx", [P, BATCH, VX])
            keep = sb("keep", [P, P])
            keep_less_1 = sb("keep_less_1", [P, P])
            sT = sb("sT", [P, BATCH, P])
            sTm = sb("sTm", [P, BATCH, P])
            state = sb("state", [P, BATCH, VX])
            acc = sb("acc", [P, BATCH, CH, VX])
            tail = sb("tail", [P, BATCH, CH, VX])
            later = sb("later", [P, BATCH, CH, VX])
            rden = sb("rden", [P, NT])
            x_in, aw_in = sem("a_x_in"), sem("a_w_in")
            cast_done = sem("a_cast")
            wT_done, wT_copied, wp_done, wp_copied = (sem(f"a_{n}") for n in ("wT", "wTc", "wp", "wpc"))
            link_d, stats_done, var_ready, std_ready = (sem(f"a_{n}") for n in ("link", "stats", "var", "std"))
            hn_ready, t_done, hT_ready, g_done, v_done = (sem(f"a_{n}") for n in ("hn", "t", "hT", "g", "v"))
            gT_ready, vx_ready, s_done, sT_ready, sTm_ready = (sem(f"a_{n}") for n in ("gT", "vx", "s", "sT", "sTm"))
            bd_done, o_done, o_stored, state_ready, ones_ready = (
                sem(f"a_{n}") for n in ("bd", "o", "os", "state", "ones"))
            fin, zero_ready = sem("a_fin"), sem("a_zero")

            with nc.Block() as block:
                @block.sync
                def _(sp):
                    xt = x.rearrange("b (t p) c -> p (b t) c", p=P)
                    sp.dma_start(X[:], xt).then_inc(x_in, 16)
                    sp.dma_start(tab[:], consts).then_inc(const_in, 16)
                    for n, w in enumerate((a_wq, a_wk, a_wv, a_wo)):
                        sp.dma_start(aw[:, n, :], w).then_inc(aw_in, 16)
                    sp.dma_start(abo_sb[:], a_bo.partition_broadcast(P)).then_inc(aw_in, 16)
                    sp.dma_start(rw_sb[:], router_w).then_inc(bw_in, 16)
                    sp.dma_start(rb_sb[:], router_b.partition_broadcast(P)).then_inc(bw_in, 16)
                    for n, w in enumerate((b_wq, b_wk, b_wv, b_wo)):
                        sp.dma_start(bw_sb[:, n, :], w).then_inc(bw_in, 16)
                    for n, v in enumerate((b_bq, b_bk)):
                        sp.dma_start(bcol[:, n:n + 1], v.rearrange("(c o) -> c o", o=1)).then_inc(bw_in, 16)
                    for n, v in enumerate((b_bv, b_bo, b_gamma, b_beta)):
                        sp.dma_start(brow[:, n, :], v.partition_broadcast(P)).then_inc(bw_in, 16)
                    sp.wait_ge(zero_ready, 1)
                    sp.dma_start(slots_dram.rearrange("(n p) c -> p n c", p=P),
                                 zero_pad[:].unsqueeze(1).broadcast_to([P, BLOCKS, P])).then_inc(pad_in, 16)
                    sp.dma_start(w1_sb[:], w1.rearrange("e c n -> c e n")).then_inc(w1_in, 16)
                    sp.dma_start(w2_sb[:], w2.rearrange("e (j p) c -> p e j c", p=P)).then_inc(w2_in, 16)

                @block.gpsimd
                def _(pool):
                    pool.memset(zero_pad[:], 0.0).then_inc(zero_ready, 1)
                    pool.memset(neg_ones[:], -1.0)
                    pool.memset(ones_bf[:], 1.0)
                    pool.memset(vx[:], 1.0).then_inc(ones_ready, 1)
                    pool.wait_ge(x_in, 16)
                    pool.wait_ge(cast_done, 4)
                    with pool.Fori(0, CH) as i:
                        for b in range(BATCH):
                            n = i * 2 + b + 1
                            pool.wait_ge(sT_ready, n)
                            pool.tensor_tensor(sTm[:, b, :], sT[:, b, :], keep_less_1[:], ALU.add
                                               ).then_inc(sTm_ready, 1)

                @block.vector
                def _(dve):
                    link = linker(dve, link_d)
                    dve.wait_ge(const_in, 16)
                    dve.tensor_copy(ident_bf[:], ident).then_inc(cast_done, 1)
                    dve.tensor_copy(before_bf[:], before).then_inc(cast_done, 1)
                    link(dve.tensor_tensor(keep[:], before, ident, ALU.add))
                    dve.tensor_scalar(keep_less_1[:], keep[:], 1.0, None, ALU.subtract).then_inc(cast_done, 2)
                    for b in range(BATCH):
                        dve.memset(state[:, b, :], 0.0).then_inc(state_ready, 1)
                    dve.wait_ge(x_in, 16)
                    norm_stats(dve, link, X, stats_done, var_ready, std_ready)
                    dve.wait_ge(ones_ready, 1)
                    with dve.Fori(0, CH) as i:
                        for b in range(BATCH):
                            t = i + b * CH
                            dve.tensor_scalar(hn[:, b, :], tile_of(X, t), mean[:, bass.ds(t, 1)],
                                              rstd[:, bass.ds(t, 1)], ALU.subtract, ALU.mult
                                              ).then_inc(hn_ready, 1)
                        for b in range(BATCH):
                            dve.wait_ge(v_done, i * 2 + b + 1)
                            dve.tensor_copy(vx[:, b, 0:P], banks[4 * b + 2][:, 0:P]).then_inc(vx_ready, 1)
                        for b in range(BATCH):
                            dve.wait_ge(s_done, i * 2 + b + 1)
                            dve.tensor_tensor(sT[:, b, :], banks[4 * b][:, 0:P], keep[:], ALU.mult
                                              ).then_inc(sT_ready, 1)
                        for b in range(BATCH):
                            n = i * 2 + b + 1
                            dve.wait_ge(bd_done, n)
                            dve.tensor_copy(tail[:, b, bass.ds(i, 1), :].rearrange("p a c -> p (a c)"),
                                            banks[4 * b + 3][:, 0:VX]).then_inc(fin, 1)
                        for b in range(BATCH):
                            n = i * 2 + b + 1
                            dve.wait_ge(o_done, n)
                            dve.tensor_copy(acc[:, b, bass.ds(i, 1), :].rearrange("p a c -> p (a c)"),
                                            banks[4 * b + 1][:, 0:VX]).then_inc(o_stored, 1)
                            dve.tensor_tensor(state[:, b, :], banks[4 * b + 3][:, VX:2 * VX],
                                              state[:, b, :], ALU.add).then_inc(state_ready, 1)
                    dve.wait_ge(fin, BATCH * CH)
                    dve.wait_ge(o_stored, BATCH * CH)
                    link(dve.memset(later[:, :, CH - 1, :], 0.0))
                    for c in range(CH - 2, -1, -1):
                        link(dve.tensor_tensor(later[:, :, c, :], later[:, :, c + 1, :], tail[:, :, c + 1, :],
                                               ALU.add))
                    accf = acc[:].rearrange("p b c v -> p (b c) v")
                    link(dve.tensor_tensor(accf, accf, later[:].rearrange("p b c v -> p (b c) v"), ALU.add))
                    link(dve.tensor_scalar(rden[:], accf[:, :, P], 1e-5, None, ALU.add))
                    link(dve.reciprocal(rden[:], rden[:]))
                    link(dve.tensor_tensor(work[:], accf[:, :, 0:P], rden[:].unsqueeze(2).broadcast_to([P, NT, P]),
                                           ALU.mult))
                    link(dve.tensor_tensor(work[:], work[:], abo_sb[:].unsqueeze(1).broadcast_to([P, NT, P]),
                                           ALU.add))
                    link(dve.tensor_tensor(X[:], X[:], work[:], ALU.add))

                @block.scalar
                def _(act):
                    act.wait_ge(wT_done, 1)
                    act.activation(woT[:], banks[0][:, 0:P], ACT.Copy).then_inc(wT_copied, 1)
                    act.wait_ge(wp_done, 1)
                    act.activation(gmat[:], banks[1][:, 0:P], ACT.Copy, scale=0.01).then_inc(wp_copied, 1)
                    act.activation(vmat[:], banks[1][:, P:2 * P], ACT.Copy).then_inc(wp_copied, 1)
                    norm_sqrt(act, var_ready, std_ready)
                    with act.Fori(0, CH) as i:
                        for b in range(BATCH):
                            act.wait_ge(t_done, i * 2 + b + 1)
                            act.activation(hT[:, b, :], banks[4 * b][:, 0:P], ACT.Copy).then_inc(hT_ready, 1)
                        for b in range(BATCH):
                            act.wait_ge(g_done, i * 2 + b + 1)
                            act.activation(gT[:, b, :], banks[4 * b + 1][:, 0:P], ACT.Copy).then_inc(gT_ready, 1)

                @block.tensor
                def _(pe):
                    pe.wait_ge(const_in, 16)
                    pe.wait_ge(aw_in, 16 * 5)
                    pe.transpose(banks[0][:, 0:P], aw[:, 3, :], ident).then_inc(wT_done, 1)
                    pe.matmul(banks[1][:, 0:P], aw[:, 0, :], aw[:, 1, :], start=True, stop=True)
                    pe.wait_ge(wT_copied, 1)
                    pe.matmul(banks[1][:, P:2 * P], aw[:, 2, :], woT[:], start=True, stop=True
                              ).then_inc(wp_done, 1)
                    pe.wait_ge(wp_copied, 2)
                    pe.wait_ge(ones_ready, 1)
                    with pe.Fori(0, CH) as i:
                        for b in range(BATCH):
                            pe.wait_ge(hn_ready, i * 2 + b + 1)
                            pe.transpose(banks[4 * b][:, 0:P], hn[:, b, :], ident).then_inc(t_done, 1)
                        for b in range(BATCH):
                            n = i * 2 + b + 1
                            pe.wait_ge(hT_ready, n)
                            pe.wait_ge(state_ready, n)
                            pe.matmul(banks[4 * b + 1][:, 0:P], gmat[:], hT[:, b, :], start=True, stop=True
                                      ).then_inc(g_done, 1)
                            pe.matmul(banks[4 * b + 2][:, 0:P], hT[:, b, :], vmat[:], start=True, stop=True
                                      ).then_inc(v_done, 1)
                        for b in range(BATCH):
                            pe.wait_ge(gT_ready, i * 2 + b + 1)
                            pe.matmul(banks[4 * b][:, 0:P], hT[:, b, :], gT[:, b, :], start=True, stop=True
                                      ).then_inc(s_done, 1)
                        for b in range(BATCH):
                            pe.wait_ge(vx_ready, i * 2 + b + 1)
                            pe.matmul(banks[4 * b + 3][:, 0:VX], neg_ones[:], vx[:, b, :], start=True, stop=True)
                            pe.matmul(banks[4 * b + 3][:, VX:2 * VX], hn[:, b, :], vx[:, b, :],
                                      start=True, stop=True).then_inc(bd_done, 1)
                        for b in range(BATCH):
                            pe.matmul(banks[4 * b + 1][:, 0:VX], gT[:, b, :], state[:, b, :],
                                      start=True, stop=False)
                            pe.wait_ge(sTm_ready, i * 2 + b + 1)
                            pe.matmul(banks[4 * b + 1][:, 0:VX], sTm[:, b, :], vx[:, b, :],
                                      start=False, stop=True).then_inc(o_done, 1)

        slot_i = sb("slot_i", [P, NT], I32)
        prob = sb("prob", [P, NT])

        def experts(layer, own_sb):
            tag = f"f{layer}"

            def sb(name, shape, dt=F32):
                return own_sb(f"{tag}_{name}", shape, dt)

            hT_g = sb("hT_g", [P, 2, 4 * P])
            logit = sb("logit", [P, NT, EXPERTS])
            rt_a = sb("rt_a", [P, NT, EXPERTS])
            onehot = sb("onehot", [P, NT, EXPERTS])
            onehot_bf = sb("onehot_bf", [P, NT, EXPERTS], BF16)
            top = sb("top", [P, NT])
            slot_f = sb("slot_f", [P, NT])
            cnt = sb("cnt", [P, EXPERTS])
            cmp16 = sb("cmp16", [P, EXPERTS, NT])
            nblk = sb("nblk", [P, EXPERTS])
            cmp8 = sb("cmp8", [P, EXPERTS, EXPERTS])
            ends = sb("ends", [P, EXPERTS])
            cmpb = sb("cmpb", [1, BLOCKS, EXPERTS])
            owner_f = sb("owner_f", [1, BLOCKS])
            owner = sb("owner", [1, BLOCKS], I32)
            xin = sb("xin", [P, 2, P])
            xT = sb("xT", [P, 2, P])
            up = sb("up", [P, 2, FFN])
            gated = sb("gated", [P, 2, FFN])
            gatedT = sb("gatedT", [P, 2, FFN])
            yout = sb("yout", [P, 2, P])
            link_d, stats_done, var_ready, std_ready, h_ready = (
                sem(f"{tag}_{n}") for n in ("link", "stats", "var", "std", "h"))
            t_done, t_copied, l_done, e_in, e_done, oh_ready, r_done, slots_ready = (
                sem(f"{tag}_{n}") for n in ("t", "tc", "l", "ei", "e", "oh", "r", "slot"))

            xin_ready = [sem(f"{tag}_xin{s}") for s in range(2)]
            y_out = [sem(f"{tag}_yout{s}") for s in range(2)]
            xt_done, xT_ready, up_done, up_ready, gated_ready, gt_done, gT_ready, y_done, y_ready = (
                sem(f"{tag}_{n}") for n in ("xt", "xT", "up", "upr", "gat", "gt", "gTr", "y", "yr"))

            def steps(eng, body):
                for n in range(2):
                    body(n, n, 0)
                with eng.Fori(1, BLOCKS // 2 - 1) as i:
                    for k in range(2):
                        body(i * 2 + k, k, i)
                for n in range(BLOCKS // 2 * 2 - 2, BLOCKS + 2):
                    body(n, n % 2, n // 2)

            def inside(n, lo=0):
                return not isinstance(n, int) or lo <= n < BLOCKS

            with nc.Block() as block:
                @block.vector
                def _(dve):
                    link = linker(dve, link_d)
                    norm_stats(dve, link, X, stats_done, var_ready, std_ready)
                    for t in range(NT):
                        normed(dve, H[:, t, :], X[:, t, :], t).then_inc(h_ready, 1)
                    dve.wait_ge(l_done, 1)
                    link(dve.tensor_tensor(logit[:], banks[2][:, 0:NT * EXPERTS].rearrange("p (t e) -> p t e", t=NT),
                                           rb_sb[:].unsqueeze(1).broadcast_to([P, NT, EXPERTS]), ALU.add))
                    link(dve.tensor_reduce(top[:], logit[:], AX_X, ALU.max))
                    topb = top[:].unsqueeze(2).broadcast_to([P, NT, EXPERTS])
                    revb = rank_rev.unsqueeze(1).broadcast_to([P, NT, EXPERTS])
                    dve.tensor_tensor(rt_a[:], logit[:], topb, ALU.subtract).then_inc(e_in, 1)
                    link(dve.tensor_tensor(onehot[:], logit[:], topb, ALU.is_equal))
                    link(dve.tensor_tensor(onehot[:], onehot[:], revb, ALU.mult))
                    link(dve.tensor_reduce(slot_f[:], onehot[:], AX_X, ALU.max))
                    link(dve.tensor_tensor(onehot[:], revb, slot_f[:].unsqueeze(2).broadcast_to([P, NT, EXPERTS]),
                                           ALU.is_equal))
                    dve.tensor_copy(onehot_bf[:], onehot[:]).then_inc(oh_ready, 1)
                    dve.wait_ge(e_done, 1)
                    link(dve.tensor_reduce(prob[:], rt_a[:], AX_X, ALU.add))
                    link(dve.reciprocal(prob[:], prob[:]))
                    dve.wait_ge(r_done, 1)
                    link(dve.tensor_reduce(cnt[:], banks[4][:, 0:NT * EXPERTS].rearrange("p (t e) -> p e t", t=NT),
                                           AX_X, ALU.add))
                    link(dve.tensor_tensor(cmp16[:], cnt[:].unsqueeze(2).broadcast_to([P, EXPERTS, NT]),
                                           thresholds.unsqueeze(1).broadcast_to([P, EXPERTS, NT]), ALU.is_gt))
                    link(dve.tensor_reduce(nblk[:], cmp16[:], AX_X, ALU.add))
                    link(dve.tensor_tensor(cmp8[:], nblk[:].unsqueeze(1).broadcast_to([P, EXPERTS, EXPERTS]),
                                           upto.rearrange("p (a b) -> p a b", a=EXPERTS), ALU.mult))
                    link(dve.tensor_reduce(ends[:], cmp8[:], AX_X, ALU.add))
                    link(dve.tensor_tensor(cmpb[:], ends[0:1, :].unsqueeze(1).broadcast_to([1, BLOCKS, EXPERTS]),
                                           block_no[0:1, :].unsqueeze(2).broadcast_to([1, BLOCKS, EXPERTS]),
                                           ALU.is_le))
                    link(dve.tensor_reduce(owner_f[:], cmpb[:], AX_X, ALU.add))
                    link(dve.tensor_scalar(owner[:], owner_f[:], float(EXPERTS - 1), None, ALU.min))
                    link(dve.tensor_tensor(ends[:], ends[:], nblk[:], ALU.subtract))
                    link(dve.tensor_scalar(ends[:], ends[:], float(P), None, ALU.mult))
                    link(dve.tensor_tensor(rt_a[:], banks[3][:, 0:NT * EXPERTS].rearrange("p (t e) -> p t e", t=NT),
                                           ends[:].unsqueeze(1).broadcast_to([P, NT, EXPERTS]), ALU.add))
                    link(dve.tensor_tensor(rt_a[:], rt_a[:], onehot[:], ALU.mult))
                    link(dve.tensor_reduce(slot_f[:], rt_a[:], AX_X, ALU.add))
                    dve.tensor_copy(slot_i[:], slot_f[:]).then_inc(slots_ready, 1)

                    def step(n, s, stored):
                        if inside(n + 1):
                            dve.wait_ge(xt_done, n + 2)
                            dve.tensor_copy(xT[:, 1 - s, :], banks[5][:, 0:P]).then_inc(xT_ready, 1)
                        if inside(n):
                            dve.wait_ge(up_ready, n + 1)
                            dve.tensor_tensor(gated[:, s, :], banks[2 * s + 1][:], up[:, s, :], ALU.mult
                                              ).then_inc(gated_ready, 1)
                        if inside(n - 2):
                            dve.wait_ge(y_done, n - 1)
                            if inside(n - 2, 2):
                                dve.wait_ge(y_out[s], (stored - 1) * 16)
                            dve.tensor_copy(yout[:, s, :], banks[6][:, 0:P]).then_inc(y_ready, 1)

                    dve.wait_ge(xt_done, 1)
                    dve.tensor_copy(xT[:, 0, :], banks[5][:, 0:P]).then_inc(xT_ready, 1)
                    steps(dve, step)
                    for g in range(4):
                        dve.wait_ge(gathered[g], 16 * 4 * (layer + 1))
                        for t in range(4 * g, 4 * g + 4):
                            dve.scalar_tensor_tensor(X[:, t, :], work[:, t, :], prob[:, t:t + 1], X[:, t, :],
                                                     ALU.mult, ALU.add).then_inc(x_done, 1)

                @block.scalar
                def _(act):
                    norm_sqrt(act, var_ready, std_ready)
                    for g in range(NT // 4):
                        act.wait_ge(t_done, g + 1)
                        act.activation(hT_g[:, g % 2, :], banks[g % 2][:], ACT.Copy).then_inc(t_copied, 1)
                    act.wait_ge(e_in, 1)
                    act.activation(rt_a[:], rt_a[:], ACT.Exp).then_inc(e_done, 1)

                    def step(n, s, stored):
                        if inside(n):
                            act.wait_ge(up_done, n + 1)
                            act.activation(up[:, s, :], banks[2 * s][:], ACT.Silu).then_inc(up_ready, 1)
                        if inside(n - 1):
                            act.wait_ge(gt_done, n)
                            act.activation(gatedT[:, 1 - s, :], banks[4][:], ACT.Copy).then_inc(gT_ready, 1)

                    steps(act, step)

                @block.tensor
                def _(pe):
                    pe.wait_ge(bw_in, 16 * 12)

                    def logits(g):
                        pe.wait_ge(t_copied, g + 1)
                        for k in range(4):
                            t = 4 * g + k
                            last = pe.matmul(banks[2][:, t * EXPERTS:(t + 1) * EXPERTS],
                                             hT_g[:, g % 2, k * P:(k + 1) * P], rw_sb[:], start=True, stop=True)
                        if g == NT // 4 - 1:
                            last.then_inc(l_done, 1)

                    for g in range(NT // 4):
                        pe.wait_ge(h_ready, 4 * g + 4)
                        for k in range(4):
                            last = pe.transpose(banks[g % 2][:, k * P:(k + 1) * P], H[:, 4 * g + k, :], ident)
                        last.then_inc(t_done, 1)
                        if g:
                            logits(g - 1)
                    logits(NT // 4 - 1)
                    pe.wait_ge(oh_ready, 1)
                    ohf = onehot_bf[:].rearrange("p t e -> p (t e)")
                    pe.matmul(banks[4][:, 0:NT * EXPERTS], ones_bf[:], ohf, start=True, stop=True)
                    pe.matmul(banks[3][:, 0:NT * EXPERTS], before_bf[:], ohf, start=True, stop=False)
                    for t in range(NT - 1):
                        last = pe.matmul(banks[3][:, (t + 1) * EXPERTS:NT * EXPERTS], ones_bf[:],
                                         onehot_bf[:, t:t + 1, :].broadcast_to([P, NT - 1 - t, EXPERTS]),
                                         start=False, stop=(t == NT - 2))
                    last.then_inc(r_done, 1)
                    pe.wait_ge(w1_in, 16)
                    pe.wait_ge(w2_in, 16)

                    def expert_of(n):
                        return pe.value_load(owner[0:1, bass.ds(n, 1)], min_val=0, max_val=EXPERTS - 1)

                    def enter(s, use):
                        pe.wait_ge(xin_ready[s], use * 16)
                        pe.transpose(banks[5][:, 0:P], xin[:, s, :], ident).then_inc(xt_done, 1)

                    def step(n, s, stored):
                        if inside(n):
                            e = expert_of(n)
                            pe.wait_ge(xT_ready, n + 1)
                            for half in range(2):
                                last = pe.matmul(banks[2 * s + half][:], xT[:, s, :],
                                                 w1_sb[:, bass.ds(e, 1), half * FFN:(half + 1) * FFN]
                                                 .rearrange("p a n -> p (a n)"), start=True, stop=True)
                            last.then_inc(up_done, 1)
                        if inside(n + 1):
                            enter(1 - s, stored + 1 + s)
                        if inside(n - 1):
                            pe.wait_ge(gated_ready, n)
                            if inside(n - 1, 1):
                                pe.wait_ge(gT_ready, n - 1)
                            for j in range(FJ):
                                last = pe.transpose(banks[4][:, j * P:(j + 1) * P],
                                                    gated[:, 1 - s, j * P:(j + 1) * P], ident)
                            last.then_inc(gt_done, 1)
                        if inside(n - 2):
                            e = expert_of(n - 2)
                            pe.wait_ge(gT_ready, n - 1)
                            if inside(n - 2, 1):
                                pe.wait_ge(y_ready, n - 2)
                            for j in range(FJ):
                                last = pe.matmul(banks[6][:, 0:P], gatedT[:, s, j * P:(j + 1) * P],
                                                 w2_sb[:, bass.ds(e, 1), j, :].rearrange("p a n -> p (a n)"),
                                                 start=(j == 0), stop=(j == FJ - 1))
                            last.then_inc(y_done, 1)

                    enter(0, 1)
                    steps(pe, step)

                @block.gpsimd
                def _(pool):
                    pool.wait_ge(pad_in, 16)
                    pool.wait_ge(slots_ready, 1)
                    pool.wait_ge(h_ready, NT)
                    for t in range(NT):
                        pool.indirect_dma_start(slots_dram, bass.IndirectOffsetOnAxis(slot_i[:, t:t + 1], 0),
                                                H[:, t, :], None).then_inc(scattered, 16)
                    pool.wait_ge(y_out[0], 16 * (BLOCKS - BLOCKS // 2))
                    pool.wait_ge(y_out[1], 16 * (BLOCKS // 2))
                    for t in range(NT):
                        pool.indirect_dma_start(work[:, t, :], None, ys_dram,
                                                bass.IndirectOffsetOnAxis(slot_i[:, t:t + 1], 0)
                                                ).then_inc(gathered[t // 4], 16)

                @block.sync
                def _(sp):
                    sp.wait_ge(scattered, 16 * NT * (layer + 1))
                    for s in range(2):
                        sp.dma_start(xin[:, s, :], slots_dram[s * P:(s + 1) * P, :]).then_inc(xin_ready[s], 16)

                    def step(n, s, stored):
                        if inside(n + 2):
                            sp.wait_ge(xt_done, n + 1)
                            sp.dma_start(xin[:, s, :], slots_dram[bass.ds((n + 2) * P, P), :]
                                         ).then_inc(xin_ready[s], 16)
                        if inside(n - 2):
                            sp.wait_ge(y_ready, n - 1)
                            sp.dma_start(ys_dram[bass.ds((n - 2) * P, P), :], yout[:, s, :]).then_inc(y_out[s], 16)

                    steps(sp, step)

        def softmax_attention(stack):
            sb = own(stack)
            ctxb = sb("ctxb", [P, NT, P])
            vall = sb("vall", [P, BATCH, KT, P])
            hT_g = sb("b_hT", [P, 2, 4 * P])

            def project(sb):
                full = sb("full", [P, 2, 2, QH])
                rest = sb("rest", [P, 2, 2, QH])
                parts = sb("parts", [P, 2, 2, PARTS, QH], BF16)
                zero_one = sb("zero_one", [P, 2, SEQ], BF16)
                link_d, stats_done, var_ready, std_ready, h_ready = (
                    sem(f"b_{n}") for n in ("link", "stats", "var", "std", "h"))
                t_done, t_copied, qk_done, v_done, head_ready, rest_ready, mid_ready, low_ready, v_ready = (
                    sem(f"b_{n}") for n in ("t", "tc", "qk", "v", "hd", "rs", "md", "lw", "vr"))
                rows_ready, rows_out = sem("b_rows"), sem("b_rows_out")
                parts_out = [[sem(f"b_out{o}{s}") for s in range(2)] for o in range(2)]
                NG = NT // 4

                with nc.Block() as block:
                    @block.gpsimd
                    def _(pool):
                        pool.memset(zero_one[:, 0, :], 0.0).then_inc(rows_ready, 1)
                        pool.memset(zero_one[:, 1, :], 1.0).then_inc(rows_ready, 1)

                    @block.vector
                    def _(dve):
                        link = linker(dve, link_d)
                        norm_stats(dve, link, X, stats_done, var_ready, std_ready)
                        for t in range(NT):
                            normed(dve, H[:, t, :], X[:, t, :], t).then_inc(h_ready, 1)

                        def split(n):
                            g, o = n // 2, n % 2
                            dve.wait_ge(head_ready, n + 1)
                            dve.tensor_tensor(rest[:, o, g % 2, :], full[:, o, g % 2, :],
                                              parts[:, o, g % 2, 0, :], ALU.subtract).then_inc(rest_ready, 1)

                        def low(n):
                            g, o = n // 2, n % 2
                            dve.wait_ge(mid_ready, n + 1)
                            dve.tensor_tensor(parts[:, o, g % 2, 2, :], rest[:, o, g % 2, :],
                                              parts[:, o, g % 2, 1, :], ALU.subtract).then_inc(low_ready, 1)

                        for n in range(2 * NG):
                            g = n // 2
                            split(n)
                            if n:
                                low(n - 1)
                            if n % 2:
                                dve.wait_ge(v_done, g + 1)
                                dve.tensor_tensor(vall[:, g // 2, g % 2 * 4:g % 2 * 4 + 4, :],
                                                  banks[4 + 3 * (g % 2)].rearrange("p (t c) -> p t c", t=4),
                                                  brow[:, 0:1, :].broadcast_to([P, 4, P]), ALU.add
                                                  ).then_inc(v_ready, 1)
                        low(2 * NG - 1)

                    @block.scalar
                    def _(act):
                        norm_sqrt(act, var_ready, std_ready)

                        def turned(g):
                            act.wait_ge(t_done, g + 1)
                            act.activation(hT_g[:, g % 2, :], banks[g % 2], ACT.Copy).then_inc(t_copied, 1)

                        def head(n):
                            g, o = n // 2, n % 2
                            act.wait_ge(qk_done, n + 1)
                            if g >= 2:
                                act.wait_ge(parts_out[o][g % 2], 16 * len(PRODUCTS) * (g // 2))
                                act.wait_ge(low_ready, n - 3)
                            src = banks[2 + o + 3 * (g % 2)]
                            act.activation(full[:, o, g % 2, :], src, ACT.Identity, bias=bcol[:, o:o + 1])
                            act.activation(parts[:, o, g % 2, 0, :], src, ACT.Identity,
                                           bias=bcol[:, o:o + 1]).then_inc(head_ready, 1)

                        def middle(n):
                            g, o = n // 2, n % 2
                            act.wait_ge(rest_ready, n + 1)
                            act.activation(parts[:, o, g % 2, 1, :], rest[:, o, g % 2, :], ACT.Copy
                                           ).then_inc(mid_ready, 1)

                        turned(0)
                        for n in range(2 * NG):
                            if n % 2 and n // 2 + 1 < NG:
                                turned(n // 2 + 1)
                            head(n)
                            if n:
                                middle(n - 1)
                        middle(2 * NG - 1)

                    @block.tensor
                    def _(pe):
                        def turn(g):
                            pe.wait_ge(h_ready, 4 * g + 4)
                            for k in range(4):
                                last = pe.transpose(banks[g % 2][:, k * P:(k + 1) * P], H[:, 4 * g + k, :], ident)
                            last.then_inc(t_done, 1)

                        turn(0)
                        for g in range(NG):
                            if g + 1 < NG:
                                turn(g + 1)
                            pe.wait_ge(t_copied, g + 1)
                            base = 2 + 3 * (g % 2)
                            for o in range(2):
                                if g >= 2:
                                    pe.wait_ge(head_ready, 2 * (g - 2) + o + 1)
                                pe.matmul(banks[base + o], bw_sb[:, o, :], hT_g[:, g % 2, :], start=True, stop=True
                                          ).then_inc(qk_done, 1)
                            if g >= 2:
                                pe.wait_ge(v_ready, g - 1)
                            for k in range(4):
                                last = pe.matmul(banks[base + 2][:, k * P:(k + 1) * P],
                                                 hT_g[:, g % 2, k * P:(k + 1) * P], bw_sb[:, 2, :],
                                                 start=True, stop=True)
                            last.then_inc(v_done, 1)

                    @block.sync
                    def _(sp):
                        sp.wait_ge(rows_ready, 2)
                        for n, stack_ in enumerate((qd, kd)):
                            sp.dma_start(stack_[:, SHIFT_ROW:SHIFT_ROW + PARTS, :],
                                         zero_one[0:BATCH * HEADS * PARTS, n, :]).then_inc(rows_out, 16)
                        for n in range(2 * NG):
                            g, o = n // 2, n % 2
                            sp.wait_ge(low_ready, n + 1)
                            b, t0 = g // 2, g % 2 * QH
                            for m, pair in enumerate(PRODUCTS):
                                dst = (qd, kd)[o][b * HEADS:(b + 1) * HEADS, PROW[m]:PROW[m] + DK, t0:t0 + QH]
                                sp.dma_start(dst, parts[:, o, g % 2, pair[o], :]).then_inc(parts_out[o][g % 2], 16)
                        sp.wait_ge(rows_out, 32)
                        for o in range(2):
                            for s in range(2):
                                sp.wait_ge(parts_out[o][s], 16 * len(PRODUCTS) * (NG // 2))

            def attend(sb):
                qst = sb("qst", [P, UNITS, 2, QH], BF16)
                kst = sb("kst", [P, BATCH, 2, SEQ], BF16)
                vst = sb("vst", [P, BATCH, KT, HG, 32])
                probs = sb("probs", [P, 4, HG, QH])
                mx = sb("mx", [P, QT, 2, HG])
                shift = sb("shift", [P, QT, HG])
                shift_rest = sb("shift_rest", [P, QT, HG])
                shift_parts = sb("shift_parts", [P, QT, HG, PARTS], BF16)
                shift_rows = sb("shift_rows", [HG * PARTS, 2, QH], BF16)
                ctxT = sb("ctxT", [P, QH])
                rden = sb("b_rden", [P, 2, QT, HG])
                q_in = [sem(f"q_in{s}") for s in range(UNITS)]
                k_in = [sem(f"k_in{b}") for b in range(BATCH)]
                shift_in = [sem(f"shift_in{s}") for s in range(UNITS)]
                v_staged = [sem(f"v_staged{b}") for b in range(BATCH)]
                act_filled, act_drained, dve_filled, dve_drained, values_done = (
                    sem(f"at_{n}") for n in ("af", "ad", "df", "dd", "values"))
                shift_link, parts_ready = sem("sh_link"), sem("sh_parts")
                ctxT_ready, rden_ready, v_clear = (sem(f"cx_{n}") for n in ("T", "rden", "vclear"))
                qsrc = qd.rearrange("(g pair r) row t -> g r row pair t", pair=2, r=2)
                ksrc = kd.rearrange("(g pair r) row t -> g r row pair t", pair=2, r=2)

                ACT_RING, DVE_RING, VALUE_BANK = 3, 4, banks[7]
                MAX_TILES = QT * 2 * HG
                PER_STEP = MAX_TILES // KT
                PER_UNIT = KT * HG + 1

                def schedule(first, last):
                    for s in range(UNITS):
                        for kt in range(KT):
                            ahead = s + 1 if kt < KT // 2 else s + 2
                            tile = (kt + KT // 2) % KT * PER_STEP
                            for j in range(HG):
                                yield "score", s, kt, j
                                if kt == 1 and j == 1 and (s or not first):
                                    yield "context", s - 1, 0, 0
                                if not (last and ahead >= UNITS):
                                    yield "max", ahead, tile + j, 0
                            if kt:
                                yield "values", s, kt - 1, 0
                            elif s or not first:
                                yield "values", s - 1, KT - 1, 0
                            if kt == 2 and (s or not first):
                                yield "turn", s - 1, 0, 0
                            if kt == 5 and not (last and s == UNITS - 1):
                                yield "rows", s + 1, 0, 0

                opening = [("max", 0, n, 0) for n in range(MAX_TILES)]
                opening += [("rows", 0, 0, 0)] + [("max", 1, n, 0) for n in range(MAX_TILES // 2)]
                closing = [("values", UNITS - 1, KT - 1, 0), ("context", UNITS - 1, 0, 0), ("turn", UNITS - 1, 0, 0)]

                def numbered(work, to_act, to_dve):
                    out, scored = [], {}
                    start = to_act
                    for kind, s, a, j in work:
                        if kind in ("score", "rows"):
                            out.append((kind, s, a, j, to_act))
                            to_act += 1
                            if kind == "score":
                                scored[s, a] = to_act
                        elif kind in ("max", "turn"):
                            out.append((kind, s, a, j, to_dve))
                            to_dve += 1
                        else:
                            out.append((kind, s, a, j, scored.get((s, a), start)))
                    return out, to_act, to_dve

                opening, to_act, to_dve = numbered(opening, 0, 0)
                first_group, to_act, to_dve = numbered(schedule(True, False), to_act, to_dve)
                middle_group, act_end, dve_end = numbered(schedule(False, False), to_act, to_dve)
                GROUP_ACT, GROUP_DVE = act_end - to_act, dve_end - to_dve
                assert GROUP_ACT % ACT_RING == 0 and GROUP_DVE % DVE_RING == 0
                last_group, act_end, dve_end = numbered(schedule(False, True), to_act + (HGROUPS - 2) * GROUP_ACT,
                                                        to_dve + (HGROUPS - 2) * GROUP_DVE)
                closing, _, _ = numbered(closing, act_end, dve_end)

                def in_group(work, i, repeat=1):
                    for kind, s, a, j, place in work:
                        size, ring = ((GROUP_DVE, DVE_RING) if kind in ("max", "turn") else (GROUP_ACT, ACT_RING))
                        slot = place % ring + (0 if ring == ACT_RING else ACT_RING)
                        place = repeat * size + (place - size) if ring == DVE_RING else place + (repeat - 1) * size
                        yield kind, i + s // UNITS, s % UNITS, i * UNITS + s, a, j, place, banks[slot]

                def rounds(eng, step):
                    for w in in_group(opening, 0):
                        step(*w)
                    for w in in_group(first_group, 0):
                        step(*w)
                    with eng.Fori(1, HGROUPS - 1) as i:
                        for w in in_group(middle_group, i, i):
                            step(*w)
                    for w in in_group(last_group, HGROUPS - 1):
                        step(*w)
                    for w in in_group(closing, HGROUPS - 1):
                        step(*w)

                def positive(n):
                    return not isinstance(n, int) or n > 0

                with nc.Block() as block:
                    @block.sync
                    def _(sp):
                        def load_q(i, s):
                            b, half = s // 2, s % 2
                            for r in range(2):
                                src = qsrc[bass.ds(i + b * HGROUPS, 1), r, :, :, half * QH:(half + 1) * QH]
                                sp.dma_start(qst[64 * r:64 * r + ROWS, s, :, :],
                                             src.rearrange("g row pair t -> (g row) pair t")).then_inc(q_in[s], 16)

                        def load_k(i, b):
                            for r in range(2):
                                src = ksrc[bass.ds(i + b * HGROUPS, 1), r, :, :, :]
                                sp.dma_start(kst[64 * r:64 * r + ROWS, b, :, :],
                                             src.rearrange("g row pair t -> (g row) pair t")).then_inc(k_in[b], 16)

                        def load_shift(count, s):
                            sp.wait_ge(act_drained, count)
                            for j in range(HG):
                                row = 64 * (j % 2) + SHIFT_ROW
                                sp.dma_start(qst[row:row + PARTS, s, j // 2, :],
                                             shift_rows[j * PARTS:(j + 1) * PARTS, s % 2, :]
                                             ).then_inc(shift_in[s], 16)

                        def group(i, last):
                            for s in range(UNITS):
                                u = i * UNITS + s
                                if not (last and s == UNITS - 1):
                                    load_shift(1 + u * PER_UNIT + 6 * HG + 1, (s + 1) % UNITS)
                                if not last:
                                    sp.wait_ge(values_done, u * KT + KT)
                                    load_q(i + 1, s)
                                    if s % 2:
                                        load_k(i + 1, s // 2)

                        load_k(0, 0)
                        load_q(0, 0)
                        load_q(0, 1)
                        load_k(0, 1)
                        load_q(0, 2)
                        load_q(0, 3)
                        load_shift(1, 0)
                        with sp.Fori(0, HGROUPS - 1) as i:
                            group(i, False)
                        group(HGROUPS - 1, True)

                    @block.gpsimd
                    def _(pool):
                        pool.memset(vst[:], 0.0).then_inc(v_clear, 1)
                        pool.wait_ge(v_clear, 1)
                        pool.memset(vst[:, :, :, :, DK:DK + 1], 1.0).then_inc(v_clear, 1)

                        def stage(i, b):
                            pool.tensor_copy(vst[:, b, :, :, 0:DK],
                                             vall[:, b, :, bass.ds(i * HG * DK, HG * DK)]
                                             .rearrange("p t (h d) -> p t h d", h=HG)).then_inc(v_staged[b], 1)

                        for b in range(BATCH):
                            stage(0, b)
                        with pool.Fori(1, HGROUPS) as i:
                            for b in range(BATCH):
                                pool.wait_ge(values_done, ((i - 1) * UNITS + 2 * b + 2) * KT)
                                stage(i, b)
                        pool.tensor_tensor(H[:], H[:], brow[:, 1:2, :].broadcast_to([P, NT, P]), ALU.add)

                    @block.vector
                    def _(dve):
                        def make_shift(u, place):
                            dve.wait_ge(dve_drained, place + 1)
                            dve.tensor_reduce(shift[:], mx[:].rearrange("p q k h -> p q h k"), AX_X, ALU.max,
                                              negate=True).then_inc(shift_link, 1)
                            dve.wait_ge(shift_link, u * 4 + 1)
                            dve.tensor_copy(shift_parts[:, :, :, 0], shift[:]).then_inc(shift_link, 1)
                            dve.wait_ge(shift_link, u * 4 + 2)
                            dve.tensor_tensor(shift_rest[:], shift[:], shift_parts[:, :, :, 0], ALU.subtract
                                              ).then_inc(shift_link, 1)
                            dve.wait_ge(shift_link, u * 4 + 3)
                            dve.tensor_copy(shift_parts[:, :, :, 1], shift_rest[:]).then_inc(shift_link, 1)
                            dve.wait_ge(shift_link, u * 4 + 4)
                            dve.tensor_tensor(shift_parts[:, :, :, 2], shift_rest[:], shift_parts[:, :, :, 1],
                                              ALU.subtract).then_inc(parts_ready, 1)

                        def step(kind, i, s, u, a, j, place, bank):
                            if kind == "max":
                                dve.wait_ge(dve_filled, place + 1)
                                dve.tensor_reduce(mx[:, a // 8, a // 4 % 2, a % 4:a % 4 + 1], bank, AX_X, ALU.max
                                                  ).then_inc(dve_drained, 1)
                                if a == MAX_TILES - 1:
                                    make_shift(u, place)
                            elif kind == "turn":
                                dve.wait_ge(dve_filled, place + 1)
                                turned = bank.rearrange("p (q h d) -> p q h d", q=QT, h=HG)
                                dve.reciprocal(rden[:, s % 2], turned[:, :, :, DK]).then_inc(rden_ready, 1)
                                dve.wait_ge(rden_ready, u + 1)
                                dve.tensor_tensor(ctxb[:, QT * s:QT * (s + 1), bass.ds(i * HG * DK, HG * DK)]
                                                  .rearrange("p q (h d) -> p q h d", h=HG),
                                                  turned[:, :, :, 0:DK],
                                                  rden[:, s % 2].unsqueeze(3).broadcast_to([P, QT, HG, DK]), ALU.mult
                                                  ).then_inc(dve_drained, 1)

                        rounds(dve, step)

                    @block.scalar
                    def _(act):
                        def step(kind, i, s, u, a, j, place, bank):
                            if kind == "score":
                                act.wait_ge(act_filled, place + 1)
                                if j == 0 and positive(u * KT + a - 3):
                                    act.wait_ge(values_done, u * KT + a - 3)
                                act.activation(probs[:, a % 4, j, :], bank, ACT.Exp, scale=SCALE
                                               ).then_inc(act_drained, 1)
                            elif kind == "rows":
                                act.wait_ge(act_filled, place + 1)
                                act.activation(shift_rows[:, s % 2, :], bank[0:HG * PARTS, :].bitcast(BF16)[:, 0:QH],
                                               ACT.Copy).then_inc(act_drained, 1)
                            elif kind == "context":
                                act.wait_ge(values_done, u * KT + KT)
                                act.activation(ctxT[:], VALUE_BANK, ACT.Copy).then_inc(ctxT_ready, 1)

                        rounds(act, step)

                    @block.tensor
                    def _(pe):
                        def step(kind, i, s, u, a, j, place, bank):
                            b = s // 2
                            if kind == "score":
                                if a == 0 and j == 0:
                                    pe.wait_ge(shift_in[s], (i + 1) * 16 * HG)
                                if positive(place - ACT_RING + 1):
                                    pe.wait_ge(act_drained, place - ACT_RING + 1)
                                base = 64 * (j % 2)
                                pe.matmul(bank, kst[base:base + ROWS, b, j // 2, a * P:(a + 1) * P],
                                          qst[base:base + ROWS, s, j // 2, :], start=True, stop=True
                                          ).then_inc(act_filled, 1)
                            elif kind == "max":
                                if a == 0:
                                    pe.wait_ge(q_in[s], (i + 1) * 32)
                                    pe.wait_ge(k_in[b], (i + 1) * 32)
                                if positive(place - DVE_RING + 1):
                                    pe.wait_ge(dve_drained, place - DVE_RING + 1)
                                qt, kh, j = a // 8, a // 4 % 2, a % 4
                                base = 64 * (j % 2)
                                pe.matmul(bank, qst[base:base + ROWS, s, j // 2, qt * P:(qt + 1) * P],
                                          kst[base:base + ROWS, b, j // 2, kh * 512:(kh + 1) * 512],
                                          start=True, stop=True).then_inc(dve_filled, 1)
                            elif kind == "rows":
                                pe.wait_ge(parts_ready, u + 1)
                                if positive(place - ACT_RING + 1):
                                    pe.wait_ge(act_drained, place - ACT_RING + 1)
                                for qt in range(QT):
                                    last = pe.transpose(bank[0:HG * PARTS, :].bitcast(BF16)[:, qt * P:(qt + 1) * P],
                                                        shift_parts[:, qt, :, :].rearrange("p h n -> p (h n)"),
                                                        ident_bf[:])
                                last.then_inc(act_filled, 1)
                            elif kind == "turn":
                                pe.wait_ge(ctxT_ready, u + 1)
                                pe.wait_ge(dve_drained, place - DVE_RING + 1)
                                for qt in range(QT):
                                    last = pe.transpose(bank[:, qt * P:(qt + 1) * P], ctxT[:, qt * P:(qt + 1) * P],
                                                        ident)
                                last.then_inc(dve_filled, 1)
                            elif kind == "values":
                                pe.wait_ge(act_drained, place)
                                if a == 0:
                                    pe.wait_ge(v_staged[b], i + 1)
                                    if positive(u):
                                        pe.wait_ge(ctxT_ready, u)
                                for j in range(HG):
                                    last = pe.matmul(VALUE_BANK[32 * j:32 * (j + 1), :], vst[:, b, a, j, :],
                                                     probs[:, a % 4, j, :], start=(a == 0), stop=(a == KT - 1))
                                last.then_inc(values_done, 1)

                        pe.wait_ge(v_clear, 2)
                        rounds(pe, step)

            def output():
                link_d, stats_done, var_ready, std_ready = (sem(f"o_{n}") for n in ("link", "stats", "var", "std"))
                t_done, t_copied, p_done, y_ready, n_ready = (sem(f"o_{n}") for n in ("t", "tc", "p", "y", "n"))
                NG = NT // 4
                with nc.Block() as block:
                    @block.vector
                    def _(dve):
                        link = linker(dve, link_d)
                        for g in range(NG):
                            dve.wait_ge(p_done, g + 1)
                            dve.tensor_tensor(work[:, 4 * g:4 * g + 4, :],
                                              banks[2 + g % 2].rearrange("p (t c) -> p t c", t=4),
                                              H[:, 4 * g:4 * g + 4, :], ALU.add).then_inc(y_ready, 1)
                        dve.wait_ge(y_ready, NG)
                        norm_stats(dve, link, work, stats_done, var_ready, std_ready)
                        for t in range(NT):
                            normed(dve, H[:, t, :], work[:, t, :], t).then_inc(n_ready, 1)
                        dve.wait_ge(n_ready, NT)
                        link(dve.tensor_tensor(H[:], H[:], brow[:, 2:3, :].broadcast_to([P, NT, P]), ALU.mult))
                        link(dve.tensor_tensor(H[:], H[:], brow[:, 3:4, :].broadcast_to([P, NT, P]), ALU.add))
                        link(dve.tensor_tensor(X[:], X[:], H[:], ALU.add))

                    @block.scalar
                    def _(act):
                        for g in range(NG):
                            act.wait_ge(t_done, g + 1)
                            act.activation(hT_g[:, g % 2, :], banks[g % 2], ACT.Copy).then_inc(t_copied, 1)
                        norm_sqrt(act, var_ready, std_ready)

                    @block.tensor
                    def _(pe):
                        def turn(g):
                            for k in range(4):
                                last = pe.transpose(banks[g % 2][:, k * P:(k + 1) * P], ctxb[:, 4 * g + k, :], ident)
                            last.then_inc(t_done, 1)

                        turn(0)
                        for g in range(NG):
                            if g + 1 < NG:
                                turn(g + 1)
                            pe.wait_ge(t_copied, g + 1)
                            if g >= 2:
                                pe.wait_ge(y_ready, g - 1)
                            for k in range(4):
                                last = pe.matmul(banks[2 + g % 2][:, k * P:(k + 1) * P],
                                                 hT_g[:, g % 2, k * P:(k + 1) * P], bw_sb[:, 3, :],
                                                 start=True, stop=True)
                            last.then_inc(p_done, 1)

            with ExitStack() as inner:
                project(own(inner))
            with ExitStack() as inner:
                attend(own(inner))
            output()

        x_done = sem("x_done")
        used.clear()
        with ExitStack() as semaphores:
            scope.append(semaphores)
            with ExitStack() as stack:
                linear_attention(own(stack))
            with ExitStack() as stack:
                experts(0, own(stack))
            with nc.Block() as block:
                @block.sync
                def _(sp):
                    for s in used:
                        sp.sem_clear(s)
            scope.pop()
        with ExitStack() as stack:
            softmax_attention(stack)
        with ExitStack() as stack:
            experts(1, own(stack))
        final = sem("final")
        with nc.Block() as block:
            @block.sync
            def _(sp):
                sp.dma_start(out.rearrange("b (t p) c -> p (b t) c", p=P), X[:]).then_inc(final, 16)
                sp.wait_ge(final, 16)


_INS = ["L0_attn_a_x", "L0_attn_a_Wq", "L0_attn_a_Wk", "L0_attn_a_Wv", "L0_attn_a_Wo", "L0_attn_a_bo",
        "L0_attn_b_Wq", "L0_attn_b_bq", "L0_attn_b_Wk", "L0_attn_b_bk", "L0_attn_b_Wv", "L0_attn_b_bv",
        "L0_attn_b_Wo", "L0_attn_b_bo", "L0_attn_b_gamma", "L0_attn_b_beta", "L0_ffn_router_w",
        "L0_ffn_router_b", "L0_ffn_w1", "L0_ffn_w2"]


def kernel(**inputs):
    import numpy as np
    import concourse.bacc as bacc
    from concourse.bass_utils import run_bass_kernel_spmd

    nc = bacc.Bacc("TRN2", target_bir_lowering=False, num_devices=1)
    arrays = {name: np.ascontiguousarray(inputs[name]) for name in _INS}
    arrays["shape_tables"] = constants()
    args = [nc.dram_tensor(name, a.shape, mybir.dt.from_np(a.dtype), kind="ExternalInput").ap()
            for name, a in arrays.items()]
    out = nc.dram_tensor("out", inputs["L0_attn_a_x"].shape, F32, kind="ExternalOutput").ap()
    hybrid_layer(nc, *args, out)
    r = run_bass_kernel_spmd(nc, [arrays], core_ids=[0])
    return r.results[0]["out"]
```

```python
from contextlib import ExitStack

import concourse.bass as bass
from concourse import mybir

F32 = mybir.dt.float32
BF16 = mybir.dt.bfloat16
I32 = mybir.dt.int32
ACT = mybir.ActivationFunctionType
ALU = mybir.AluOpType
AX_X = mybir.AxisListType.X

P = 128
BATCH, SEQ = 2, 1024
NT = BATCH * SEQ // P
CH = SEQ // P
LN_EPS = 1e-5
EXPERTS, FFN = 8, 512
FJ = FFN // P
BLOCKS = NT + EXPERTS - 1
HEADS, DK = 16, 8
HG = 4
QH = 512
PARTS = 3
PRODUCTS = [(a, b) for a in range(PARTS) for b in range(PARTS - a)]
PROWS = len(PRODUCTS) * DK
SHIFT_ROW = 2 * PROWS
ROWS = SHIFT_ROW + PARTS
SCALE = (1.0 / DK) ** 0.5
HGROUPS = HEADS // HG
UNITS = BATCH * SEQ // QH
KT = SEQ // P
QT = QH // P


def constants():
    import numpy as np
    p = np.arange(P)
    e = np.arange(EXPERTS)
    rows = [
        np.eye(P),
        (p[:, None] < p[None, :]),
        np.tile(EXPERTS - e, (P, 1)),
        np.tile(P * np.arange(NT), (P, 1)),
        np.tile((e[None, :] <= e[:, None]).reshape(1, -1), (P, 1)),
        np.tile(np.arange(BLOCKS), (P, 1)),
        p[:, None] + P * np.arange(NT)[None, :],
        p[:, None] + P * (NT + np.arange(BLOCKS))[None, :],
    ]
    return np.ascontiguousarray(np.concatenate(rows, axis=1).astype(np.float32))


CONST_COLS = 2 * P + EXPERTS + NT + EXPERTS * EXPERTS + BLOCKS + NT + BLOCKS
ROW = P + 1


def hybrid_layer(nc, x, a_wq, a_wk, a_wv, a_wo, a_bo, b_wq, b_bq, b_wk, b_bk, b_wv, b_bv, b_wo, b_bo,
                 b_gamma, b_beta, router_w, router_b, w1, w2, consts, out):
    with ExitStack() as ctx:
        def sb(name, shape, dt=F32):
            return ctx.enter_context(nc.sbuf_tensor(name, shape, dt))

        def sem(name):
            return ctx.enter_context(nc.semaphore(name))

        def own(stack):
            return lambda name, shape, dt=F32: stack.enter_context(nc.sbuf_tensor(name, shape, dt))

        def dram(name, shape, dt):
            return nc.dram_tensor(name, shape, dt, kind="Internal").ap()

        psum = ctx.enter_context(nc.psum_tensor("psum", [P, 8, 512], F32))
        banks = [psum[:, n, :] for n in range(8)]

        X = sb("X", [P, NT, P])
        rows = sb("rows", [P, NT, ROW])
        H = rows[:, :, 0:P]
        work = sb("work", [P, NT, P])
        tab = sb("tab", [P, CONST_COLS])
        ident = tab[:, 0:P]
        before = tab[:, P:2 * P]
        at = 2 * P
        rank_rev = tab[:, at:at + EXPERTS]
        at += EXPERTS
        thresholds = tab[:, at:at + NT]
        at += NT
        upto = tab[:, at:at + EXPERTS * EXPERTS]
        at += EXPERTS * EXPERTS
        block_no = tab[:, at:at + BLOCKS]
        at += BLOCKS
        token_no = tab[:, at:at + NT]
        at += NT
        empty_no = tab[:, at:at + BLOCKS]
        ident_bf = sb("ident_bf", [P, P], BF16)
        before_bf = sb("before_bf", [P, P], BF16)
        ones_bf = sb("ones_bf", [P, P], BF16)
        neg_ones = sb("neg_ones", [P, P])
        empty = sb("empty", [P, BLOCKS, ROW])
        w1_sb = sb("w1_sb", [P, EXPERTS, 2 * FFN])
        w2_sb = sb("w2_sb", [P, EXPERTS, FJ, P])
        rw_sb = sb("rw_sb", [P, EXPERTS])
        rb_sb = sb("rb_sb", [P, EXPERTS])
        abo_sb = sb("abo_sb", [P, P])
        bw_sb = sb("bw_sb", [P, 4, P])
        bcol = sb("bcol", [P, 2])
        brow = sb("brow", [P, 4, P])
        stats = sb("stats", [P, NT, 6])
        mean = sb("mean", [P, NT])
        var = sb("var", [P, NT])
        rstd = sb("rstd", [P, NT])
        ln_a = sb("ln_a", [P, NT])
        ln_b = sb("ln_b", [P, NT])
        shiftn = sb("shiftn", [P, NT])
        const_in = sem("const_in")
        w1_in, w2_in, bw_in = sem("w1_in"), sem("w2_in"), sem("bw_in")
        pad_in = sem("pad_in")
        scattered = sem("scattered")
        y_out = [sem(f"y_out{s}") for s in range(2)]

        slots_dram = [dram(f"slots{n}", [BLOCKS * P, ROW], F32) for n in range(2)]
        ys_dram = dram("ys", [(NT + BLOCKS) * P, P], F32)
        qd = dram("q_parts", [len(PRODUCTS), BATCH * P, SEQ], BF16)
        kd = dram("k_parts", [len(PRODUCTS), BATCH * P, SEQ], BF16)

        def steps(eng, count, body):
            for n in range(4):
                body(n, n % 2, n // 2)
            with eng.Fori(2, count // 2 - 1) as i:
                for k in range(2):
                    body(i * 2 + k, k, i)
            last_steps(count, body)

        def later_steps(eng, count, body):
            with eng.Fori(1, count // 2 - 1) as i:
                for k in range(2):
                    body(i * 2 + k, k, i)
            last_steps(count, body)

        def last_steps(count, body):
            for n in range(count // 2 * 2 - 2, count + 2):
                body(n, n % 2, n // 2)

        def within(n, count, lo=0):
            return not isinstance(n, int) or lo <= n < count

        def tile_of(t, i):
            return t[:, bass.ds(i, 1), :].rearrange("p a b -> p (a b)")

        def linker(eng, done):
            count = [0]

            def link(ins):
                count[0] += 1
                ins.then_inc(done, 1)
                eng.wait_ge(done, count[0])
            return link

        def norm_stats(dve, link, var_ready, std_ready):
            dve.tensor_tensor(ln_a[:], stats[:, :, 1], stats[:, :, 4], ALU.subtract)
            dve.tensor_tensor(ln_b[:], stats[:, :, 2], stats[:, :, 5], ALU.add)
            link(dve.tensor_tensor(mean[:], stats[:, :, 1], stats[:, :, 4], ALU.add))
            dve.scalar_tensor_tensor(ln_a[:], ln_a[:], 0.25, ln_a[:], ALU.mult, ALU.mult)
            dve.tensor_scalar(ln_b[:], ln_b[:], 1.0 / P, LN_EPS, ALU.mult, ALU.add)
            link(dve.tensor_scalar(mean[:], mean[:], 0.5, None, ALU.mult))
            link(dve.tensor_tensor(var[:], ln_b[:], ln_a[:], ALU.add))
            dve.sem_inc(var_ready, 1)
            dve.wait_ge(std_ready, 1)
            link(dve.reciprocal(rstd[:], ln_a[:]))
            link(dve.tensor_tensor(ln_b[:], rstd[:], rstd[:], ALU.mult))
            link(dve.tensor_tensor(ln_b[:], ln_b[:], var[:], ALU.mult))
            link(dve.tensor_scalar(ln_b[:], ln_b[:], -0.5, 1.5, ALU.mult, ALU.add))
            link(dve.tensor_tensor(rstd[:], rstd[:], ln_b[:], ALU.mult))

        def norm_sqrt(act, var_ready, std_ready):
            act.wait_ge(var_ready, 1)
            act.activation(ln_a[:], var[:], ACT.Sqrt).then_inc(std_ready, 1)

        def normed(dve, dst, src, t):
            return dve.tensor_scalar(dst, src, mean[:, t:t + 1], rstd[:, t:t + 1], ALU.subtract, ALU.mult)

        xT_g = sb("xT_g", [P, 2, 4 * P])

        class Router:

            def __init__(self, tag):
                self.turn_done, self.turn_copied, self.products_done = (sem(f"r{tag}_{n}") for n in ("t", "tc", "p"))
                self.stats_done, self.var_ready, self.std_ready = (
                    sem(f"r{tag}_{n}") for n in ("stats", "var", "std"))

            def on_pe(self, pe, tiles, wait):
                pe.wait_ge(bw_in, 16 * 12)

                def product(g):
                    pe.wait_ge(self.turn_copied, g + 1)
                    for k, t in enumerate(tiles(g)):
                        last = pe.matmul(banks[2][:, t * EXPERTS:(t + 1) * EXPERTS],
                                         xT_g[:, g % 2, k * P:(k + 1) * P], rw_sb[:], start=True, stop=True)
                    if g == NT // 4 - 1:
                        last.then_inc(self.products_done, 1)

                for g in range(NT // 4):
                    wait(g)
                    for k, t in enumerate(tiles(g)):
                        last = pe.transpose(banks[g % 2][:, k * P:(k + 1) * P], X[:, t, :], ident)
                    last.then_inc(self.turn_done, 1)
                    if g:
                        product(g - 1)
                    else:
                        pe.matmul(banks[3][:, 0:EXPERTS], neg_ones[:], rw_sb[:], start=True, stop=True
                                  ).then_inc(self.products_done, 1)
                product(NT // 4 - 1)

            def on_act(self, act, g):
                act.wait_ge(self.turn_done, g + 1)
                act.activation(xT_g[:, g % 2, :], banks[g % 2][:], ACT.Copy).then_inc(self.turn_copied, 1)

        def linear_attention(sb, router):
            VX = P + 1
            aw = sb("aw", [P, 4, P])
            woT = sb("woT", [P, P])
            gmat = sb("gmat", [P, P])
            vmat = sb("vmat", [P, P])
            hn = sb("hn", [P, 2, BATCH, P])
            hT = sb("hT_a", [P, 2, BATCH, P])
            gT = sb("gT", [P, 2, BATCH, P])
            vx = sb("vx", [P, 2, BATCH, VX])
            sTm = sb("sTm", [P, 2, BATCH, P])
            keep = sb("keep", [P, P])
            ones = sb("ones_a", [P, P])
            state = sb("state", [P, CH + 1, BATCH, VX])
            level = sb("level", [1, CH + 1, BATCH, VX])
            usum = sb("usum", [P, BATCH, P])
            sumT = sb("sumT", [P, BATCH])
            mr = sb("mr", [P, NT])
            msum = sb("msum", [P, BATCH])
            rden = sb("rden", [P, 2, BATCH])
            x_in, aw_in = [sem(f"a_x_in{b}") for b in range(BATCH)], sem("a_w_in")
            weights_done, weights_copied = sem("a_w"), sem("a_wc")
            link_d, stats_done, var_ready, std_ready = (sem(f"a_{n}") for n in ("link", "stats", "var", "std"))
            hn_ready, t_done, hT_ready, g_done, v_done = (sem(f"a_{n}") for n in ("hn", "t", "hT", "g", "v"))
            gT_ready, vx_ready, s_done, sTm_ready = (sem(f"a_{n}") for n in ("gT", "vx", "s", "sTm"))
            b_done, c_done, o_done, state_ready, level_ready, ones_ready = (
                sem(f"a_{n}") for n in ("b", "c", "o", "state", "level", "ones"))
            total_done, total_copied, pool_link = (sem(f"a_{n}") for n in ("total", "totalc", "pool"))
            norm_ready, usum_ready, xb_ready, rden_ready, x_new, empty_ready = (
                sem(f"a_{n}") for n in ("norm", "usum", "xb", "rden", "x_new", "empty"))
            T_BANK, V_BANK, G_BANK, S_BANK, C_BANK, B_BANK, O_BANK, TOTAL_BANK = banks

            def inside(n, lo=0):
                return within(n, CH, lo)

            def pair(bank, width=P):
                return bank[:, 0:BATCH * width].rearrange("p (b c) -> p b c", b=BATCH)

            def both(t, i):
                return t.rearrange("p (b c) v -> p b c v", b=BATCH)[:, :, bass.ds(i, 1), :].rearrange(
                    "p b c v -> p b (c v)")

            def sum_normed(eng, link, b):
                wb = work[:, b * CH:(b + 1) * CH, :]
                link(eng.tensor_tensor(wb, X[:, b * CH:(b + 1) * CH, :],
                                       rstd[:, b * CH:(b + 1) * CH].unsqueeze(2).broadcast_to([P, CH, P]), ALU.mult))
                half = CH // 2
                while half > 1:
                    link(eng.tensor_tensor(wb[:, 0:half, :], wb[:, 0:half, :], wb[:, half:2 * half, :], ALU.add))
                    half //= 2
                link(eng.tensor_tensor(usum[:, b, :], wb[:, 0, :], wb[:, 1, :], ALU.add))
                eng.tensor_tensor(usum[:, b, :], usum[:, b, :], msum[:, b:b + 1].broadcast_to([P, P]),
                                  ALU.subtract).then_inc(usum_ready, 1)

            with nc.Block() as block:
                @block.sync
                def _(sp):
                    for b in range(BATCH):
                        sp.dma_start(X[:, b * CH:(b + 1) * CH, :], x[b].rearrange("(t p) c -> p t c", p=P)
                                     ).then_inc(x_in[b], 16)
                    sp.dma_start(tab[:], consts).then_inc(const_in, 16)
                    for n, w in enumerate((a_wq, a_wk, a_wv, a_wo)):
                        sp.dma_start(aw[:, n, :], w).then_inc(aw_in, 16)
                    sp.dma_start(abo_sb[:], a_bo.partition_broadcast(P)).then_inc(aw_in, 16)
                    sp.dma_start(rw_sb[:], router_w).then_inc(bw_in, 16)
                    sp.dma_start(rb_sb[:], router_b.partition_broadcast(P)).then_inc(bw_in, 16)
                    for n, w in enumerate((b_wq, b_wk, b_wv, b_wo)):
                        sp.dma_start(bw_sb[:, n, :], w).then_inc(bw_in, 16)
                    for n, v in enumerate((b_bq, b_bk)):
                        sp.dma_start(bcol[:, n:n + 1], v.rearrange("(c o) -> c o", o=1)).then_inc(bw_in, 16)
                    for n, v in enumerate((b_bv, b_bo, b_gamma, b_beta)):
                        sp.dma_start(brow[:, n, :], v.partition_broadcast(P)).then_inc(bw_in, 16)
                    sp.wait_ge(empty_ready, 2)
                    for slots in slots_dram:
                        sp.dma_start(slots.rearrange("(n p) c -> p n c", p=P), empty[:]).then_inc(pad_in, 16)
                    sp.dma_start(w1_sb[:], w1.rearrange("e c n -> c e n")).then_inc(w1_in, 16)
                    sp.dma_start(w2_sb[:], w2.rearrange("e (j p) c -> p e j c", p=P)).then_inc(w2_in, 16)

                @block.gpsimd
                def _(pool):
                    pool.memset(empty[:], 0.0).then_inc(empty_ready, 1)
                    pool.memset(neg_ones[:], -1.0)
                    pool.memset(ones_bf[:], 1.0)
                    pool.memset(ones[:], 1.0)
                    pool.memset(state[:, 0], 0.0)
                    pool.memset(level[:, 0, :, P:VX], -float(SEQ))
                    pool.memset(vx[:], 1.0).then_inc(ones_ready, 1)
                    pool.wait_ge(const_in, 16)
                    pool.tensor_copy(rows[:, :, P], token_no)
                    pool.wait_ge(empty_ready, 1)
                    pool.tensor_copy(empty[:, :, P], empty_no).then_inc(empty_ready, 1)
                    pool.wait_ge(aw_in, 16 * 5)
                    for b in range(BATCH):
                        pool.wait_ge(x_in[b], 16)
                    pool.tensor_tensor(H, X[:], abo_sb[:].unsqueeze(1).broadcast_to([P, NT, P]), ALU.add
                                       ).then_inc(xb_ready, 1)
                    pool.wait_ge(norm_ready, 2)
                    sum_normed(pool, linker(pool, pool_link), 0)

                @block.vector
                def _(dve):
                    link = linker(dve, link_d)
                    for b in range(BATCH):
                        dve.wait_ge(x_in[b], 16)
                        for t in range(b * CH, (b + 1) * CH):
                            dve.bn_stats(stats[:, t, :], X[:, t, :]).then_inc(stats_done, 1)
                    dve.wait_ge(stats_done, NT)
                    norm_stats(dve, link, var_ready, std_ready)
                    link(dve.tensor_tensor(mr[:], mean[:], rstd[:], ALU.mult))
                    dve.sem_inc(norm_ready, 1)
                    dve.tensor_reduce(msum[:], mr[:].rearrange("p (b t) -> p b t", b=BATCH), AX_X, ALU.add
                                      ).then_inc(norm_ready, 1)

                    def norm(n, s):
                        for b in range(BATCH):
                            t = n + b * CH
                            last = dve.tensor_scalar(hn[:, s, b, :], tile_of(X, t), mean[:, bass.ds(t, 1)],
                                                     rstd[:, bass.ds(t, 1)], ALU.subtract, ALU.mult)
                        last.then_inc(hn_ready, 1)

                    def step(n, s, stored):
                        if inside(n - 1):
                            dve.wait_ge(b_done, n)
                            if inside(n - 1, 1):
                                dve.wait_ge(state_ready, n - 1)
                        if inside(n + 1):
                            norm(n + 1, 1 - s)
                        if inside(n - 1):
                            dve.tensor_tensor(state[:, bass.ds(n, 1)].rearrange("p a b v -> p (a b) v"),
                                              state[:, bass.ds(n - 1, 1)].rearrange("p a b v -> p (a b) v"),
                                              pair(B_BANK, VX), ALU.add).then_inc(state_ready, 1)
                        if inside(n - 2):
                            sums = pair(O_BANK, VX)
                            dve.wait_ge(o_done, n - 1)
                            dve.tensor_scalar(rden[:, s], sums[:, :, P], 1e-5, None, ALU.add).then_inc(rden_ready, 1)
                            dve.wait_ge(c_done, n - 1)
                            dve.wait_ge(level_ready, n - 1)
                            dve.tensor_tensor(level[:, bass.ds(n - 1, 1)].rearrange("p a b v -> p (a b) v"),
                                              level[:, bass.ds(n - 2, 1)].rearrange("p a b v -> p (a b) v"),
                                              pair(C_BANK, VX)[0:1], ALU.add).then_inc(level_ready, 1)
                            dve.wait_ge(rden_ready, (n - 1) * 2 - 1)
                            dve.reciprocal(rden[:, s], rden[:, s]).then_inc(rden_ready, 1)
                            dve.wait_ge(rden_ready, (n - 1) * 2)
                            for b in range(BATCH):
                                t = n - 2 + b * CH
                                dve.scalar_tensor_tensor(tile_of(X, t), sums[:, b, 0:P], rden[:, s, b:b + 1],
                                                         tile_of(H, t), ALU.mult, ALU.add).then_inc(x_new, 1)
                        if inside(n - 1):
                            dve.wait_ge(s_done, n)
                            dve.scalar_tensor_tensor(sTm[:, 1 - s], pair(S_BANK), 1.0,
                                                     keep[:].unsqueeze(1).broadcast_to([P, BATCH, P]),
                                                     ALU.add, ALU.mult).then_inc(sTm_ready, 1)
                        if inside(n - 2):
                            dve.wait_ge(x_new, n * BATCH)
                            for b in range(BATCH):
                                t = n - 2 + b * CH
                                last = dve.bn_stats(stats[:, bass.ds(t, 1), :].rearrange("p a b -> p (a b)"),
                                                    tile_of(X, t))
                            last.then_inc(router.stats_done, 1)

                    norm(0, 0)
                    dve.wait_ge(const_in, 16)
                    dve.tensor_copy(ident_bf[:], ident)
                    dve.tensor_copy(before_bf[:], before)
                    link(dve.tensor_tensor(keep[:], before, ident, ALU.add))
                    step(0, 0, 0)
                    dve.wait_ge(norm_ready, 2)
                    sum_normed(dve, link, 1)
                    step(1, 1, 0)
                    dve.wait_ge(total_done, 2)
                    dve.tensor_copy(level[:, 0, :, 0:P], pair(TOTAL_BANK[:, P:3 * P])[0:1]).then_inc(level_ready, 1)
                    dve.wait_ge(xb_ready, 1)
                    dve.sem_inc(x_new, BATCH)
                    later_steps(dve, CH, step)
                    dve.wait_ge(router.stats_done, CH)
                    norm_stats(dve, link, router.var_ready, router.std_ready)

                @block.scalar
                def _(act):
                    norm_sqrt(act, var_ready, std_ready)
                    act.wait_ge(weights_done, 1)
                    act.activation(woT[:], banks[0][:, 0:P], ACT.Copy).then_inc(weights_copied, 1)
                    act.wait_ge(weights_done, 2)
                    act.activation(gmat[:], banks[1][:, 0:P], ACT.Copy, scale=0.01).then_inc(weights_copied, 1)
                    act.activation(vmat[:], banks[1][:, P:2 * P], ACT.Copy).then_inc(weights_copied, 1)
                    act.wait_ge(ones_ready, 1)

                    def step(n, s, stored):
                        if inside(n):
                            act.wait_ge(t_done, n + 1)
                            act.activation(hT[:, s], pair(T_BANK), ACT.Copy).then_inc(hT_ready, 1)
                            act.wait_ge(v_done, n + 1)
                            act.activation(vx[:, s, :, 0:P], pair(V_BANK), ACT.Copy).then_inc(vx_ready, 1)
                            act.wait_ge(g_done, n + 1)
                            act.activation(gT[:, s], pair(G_BANK), ACT.Copy).then_inc(gT_ready, 1)

                    for n in range(2):
                        step(n, n, 0)
                    act.wait_ge(total_done, 1)
                    act.activation(sumT[:], TOTAL_BANK[:, 0:BATCH], ACT.Copy).then_inc(total_copied, 1)
                    later_steps(act, CH, step)
                    for g in range(NT // 4):
                        router.on_act(act, g)
                    norm_sqrt(act, router.var_ready, router.std_ready)

                @block.tensor
                def _(pe):
                    pe.wait_ge(const_in, 16)
                    pe.wait_ge(aw_in, 16 * 5)
                    pe.transpose(banks[0][:, 0:P], aw[:, 3, :], ident).then_inc(weights_done, 1)
                    pe.matmul(banks[1][:, 0:P], aw[:, 0, :], aw[:, 1, :], start=True, stop=True)
                    pe.wait_ge(weights_copied, 1)
                    pe.matmul(banks[1][:, P:2 * P], aw[:, 2, :], woT[:], start=True, stop=True
                              ).then_inc(weights_done, 1)
                    pe.wait_ge(weights_copied, 3)
                    pe.wait_ge(ones_ready, 1)

                    def step(n, s, stored):
                        if inside(n):
                            pe.wait_ge(hn_ready, n + 1)
                            if inside(n, 1):
                                pe.wait_ge(hT_ready, n)
                            for b in range(BATCH):
                                last = pe.transpose(T_BANK[:, b * P:(b + 1) * P], hn[:, s, b, :], ident)
                            last.then_inc(t_done, 1)
                        if inside(n - 1):
                            pe.wait_ge(vx_ready, n)
                            if inside(n - 1, 1):
                                pe.wait_ge(state_ready, n - 1)
                            for b in range(BATCH):
                                last = pe.matmul(B_BANK[:, b * VX:(b + 1) * VX], hn[:, 1 - s, b, :],
                                                 vx[:, 1 - s, b, :], start=True, stop=True)
                            last.then_inc(b_done, 1)
                        if inside(n - 2):
                            pe.wait_ge(level_ready, n - 1)
                            if inside(n - 2, 1):
                                pe.wait_ge(x_new, (n - 1) * BATCH)
                            pe.wait_ge(sTm_ready, n - 1)
                            for b in range(BATCH):
                                to = O_BANK[:, b * VX:(b + 1) * VX]
                                pe.matmul(to, ones[0:1, :],
                                          level[:, bass.ds(n - 2, 1), b, :].rearrange("p a v -> p (a v)"),
                                          start=True, stop=False)
                                pe.matmul(to, gT[:, s, b, :],
                                          state[:, bass.ds(n - 2, 1), b, :].rearrange("p a v -> p (a v)"),
                                          start=False, stop=False)
                                last = pe.matmul(to, sTm[:, s, b, :], vx[:, s, b, :], start=False, stop=True)
                            last.then_inc(o_done, 1)
                            pe.matmul(C_BANK[0:1, 0:BATCH * VX], ones[:, 0:1],
                                      vx[:, s].rearrange("p b v -> p (b v)"), start=True, stop=True
                                      ).then_inc(c_done, 1)
                        if inside(n):
                            pe.wait_ge(hT_ready, n + 1)
                            for b in range(BATCH):
                                last = pe.matmul(V_BANK[:, b * P:(b + 1) * P], hT[:, s, b, :], vmat[:],
                                                 start=True, stop=True)
                            last.then_inc(v_done, 1)
                            if inside(n, 1):
                                pe.wait_ge(gT_ready, n)
                            pe.matmul(G_BANK[:, 0:BATCH * P], gmat[:], hT[:, s].rearrange("p b c -> p (b c)"),
                                      start=True, stop=True).then_inc(g_done, 1)
                        if inside(n - 1):
                            pe.wait_ge(gT_ready, n)
                            if inside(n - 1, 1):
                                pe.wait_ge(sTm_ready, n - 1)
                            for b in range(BATCH):
                                last = pe.matmul(S_BANK[:, b * P:(b + 1) * P], hT[:, 1 - s, b, :],
                                                 gT[:, 1 - s, b, :], start=True, stop=True)
                            last.then_inc(s_done, 1)

                    for n in range(2):
                        step(n, n, 0)
                    pe.wait_ge(usum_ready, BATCH)
                    for b in range(BATCH):
                        last = pe.matmul(TOTAL_BANK[:, b:b + 1], usum[:, b, :], neg_ones[:, 0:1], start=True, stop=True)
                    last.then_inc(total_done, 1)
                    pe.wait_ge(total_copied, 1)
                    for b in range(BATCH):
                        last = pe.matmul(TOTAL_BANK[0:1, (b + 1) * P:(b + 2) * P], sumT[:, b:b + 1], vmat[:],
                                         start=True, stop=True)
                    last.then_inc(total_done, 1)
                    later_steps(pe, CH, step)
                    router.on_pe(pe, lambda g: [b * CH + 2 * g + k for b in range(BATCH) for k in range(2)],
                                 lambda g: pe.wait_ge(x_new, (2 * g + 3) * BATCH))

        slot_i = sb("slot_i", [P, NT], I32)
        prob = sb("prob", [P, NT])

        def experts(layer, own_sb, router):
            tag = f"f{layer}"

            def sb(name, shape, dt=F32):
                return own_sb(f"{tag}_{name}", shape, dt)

            logit = sb("logit", [P, NT, EXPERTS])
            rt_a = sb("rt_a", [P, NT, EXPERTS])
            below = sb("below", [P, NT, EXPERTS])
            onehot = sb("onehot", [P, NT, EXPERTS])
            onehot_bf = sb("onehot_bf", [P, NT, EXPERTS], BF16)
            top = sb("top", [P, NT])
            slot_f = sb("slot_f", [P, NT])
            cnt = sb("cnt", [P, EXPERTS])
            cmp16 = sb("cmp16", [P, EXPERTS, NT])
            nblk = sb("nblk", [P, EXPERTS])
            cmp8 = sb("cmp8", [P, EXPERTS, EXPERTS])
            ends = sb("ends", [P, EXPERTS])
            cmpb = sb("cmpb", [1, BLOCKS, EXPERTS])
            owner_f = sb("owner_f", [1, BLOCKS])
            owner = sb("owner", [1, BLOCKS], I32)
            xin = sb("xin", [P, 2, ROW])
            dest = sb("dest", [P, BLOCKS], I32)
            xT = sb("xT", [P, 2, P])
            up = sb("up", [P, 2, FFN])
            gated = sb("gated", [P, 2, FFN])
            gatedT = sb("gatedT", [P, 2, FFN])
            yout = sb("yout", [P, 2, P])
            link_d, h_ready = sem(f"{tag}_link"), sem(f"{tag}_h")
            e_in, e_done, oh_ready, r_done, slots_ready = (sem(f"{tag}_{n}") for n in ("ei", "e", "oh", "r", "slot"))

            xin_ready = [sem(f"{tag}_xin{s}") for s in range(2)]
            shiftn_ready = sem(f"{tag}_shiftn")
            dest_ready = sem(f"{tag}_dest")
            y_in = [sem(f"{tag}_y_in{g}") for g in range(NT // 4)]
            Y_USES = (BLOCKS - BLOCKS // 2, BLOCKS // 2)
            xt_done, xT_ready, up_done, up_ready, gated_ready, gt_done, gT_ready, y_done, y_ready = (
                sem(f"{tag}_{n}") for n in ("xt", "xT", "up", "upr", "gat", "gt", "gTr", "y", "yr"))

            def inside(n, lo=0):
                return within(n, BLOCKS, lo)

            with nc.Block() as block:
                @block.vector
                def _(dve):
                    link = linker(dve, link_d)
                    dve.scalar_tensor_tensor(shiftn[:], mean[:], -1.0, rstd[:], ALU.mult, ALU.mult
                                             ).then_inc(shiftn_ready, 1)
                    dve.wait_ge(router.products_done, 1)
                    link(dve.tensor_tensor(rt_a[:], banks[3][:, 0:EXPERTS].unsqueeze(1).broadcast_to([P, NT, EXPERTS]),
                                           mean[:].unsqueeze(2).broadcast_to([P, NT, EXPERTS]), ALU.mult))
                    dve.wait_ge(router.products_done, 2)
                    link(dve.tensor_tensor(logit[:], banks[2][:, 0:NT * EXPERTS].rearrange("p (t e) -> p t e", t=NT),
                                           rt_a[:], ALU.add))
                    link(dve.tensor_tensor(logit[:], logit[:],
                                           rstd[:].unsqueeze(2).broadcast_to([P, NT, EXPERTS]), ALU.mult))
                    link(dve.tensor_tensor(logit[:], logit[:],
                                           rb_sb[:].unsqueeze(1).broadcast_to([P, NT, EXPERTS]), ALU.add))
                    link(dve.tensor_reduce(top[:], logit[:], AX_X, ALU.max))
                    topb = top[:].unsqueeze(2).broadcast_to([P, NT, EXPERTS])
                    revb = rank_rev.unsqueeze(1).broadcast_to([P, NT, EXPERTS])
                    dve.tensor_tensor(below[:], logit[:], topb, ALU.subtract).then_inc(e_in, 1)
                    link(dve.tensor_tensor(onehot[:], logit[:], topb, ALU.is_equal))
                    link(dve.tensor_tensor(onehot[:], onehot[:], revb, ALU.mult))
                    link(dve.tensor_reduce(slot_f[:], onehot[:], AX_X, ALU.max))
                    link(dve.tensor_tensor(onehot[:], revb, slot_f[:].unsqueeze(2).broadcast_to([P, NT, EXPERTS]),
                                           ALU.is_equal))
                    dve.tensor_copy(onehot_bf[:], onehot[:]).then_inc(oh_ready, 1)
                    dve.wait_ge(r_done, 1)
                    link(dve.tensor_reduce(cnt[:], banks[4][:, 0:NT * EXPERTS].rearrange("p (t e) -> p e t", t=NT),
                                           AX_X, ALU.add))
                    link(dve.tensor_tensor(cmp16[:], cnt[:].unsqueeze(2).broadcast_to([P, EXPERTS, NT]),
                                           thresholds.unsqueeze(1).broadcast_to([P, EXPERTS, NT]), ALU.is_gt))
                    link(dve.tensor_reduce(nblk[:], cmp16[:], AX_X, ALU.add))
                    link(dve.tensor_tensor(cmp8[:], nblk[:].unsqueeze(1).broadcast_to([P, EXPERTS, EXPERTS]),
                                           upto.rearrange("p (a b) -> p a b", a=EXPERTS), ALU.mult))
                    link(dve.tensor_reduce(ends[:], cmp8[:], AX_X, ALU.add))
                    link(dve.tensor_tensor(cmpb[:], ends[0:1, :].unsqueeze(1).broadcast_to([1, BLOCKS, EXPERTS]),
                                           block_no[0:1, :].unsqueeze(2).broadcast_to([1, BLOCKS, EXPERTS]),
                                           ALU.is_le))
                    link(dve.tensor_reduce(owner_f[:], cmpb[:], AX_X, ALU.add))
                    link(dve.tensor_scalar(owner[:], owner_f[:], float(EXPERTS - 1), None, ALU.min))
                    link(dve.tensor_tensor(ends[:], ends[:], nblk[:], ALU.subtract))
                    link(dve.tensor_scalar(ends[:], ends[:], float(P), None, ALU.mult))
                    link(dve.tensor_tensor(rt_a[:], banks[3][:, 0:NT * EXPERTS].rearrange("p (t e) -> p t e", t=NT),
                                           ends[:].unsqueeze(1).broadcast_to([P, NT, EXPERTS]), ALU.add))
                    link(dve.tensor_tensor(rt_a[:], rt_a[:], onehot[:], ALU.mult))
                    link(dve.tensor_reduce(slot_f[:], rt_a[:], AX_X, ALU.add))
                    dve.tensor_copy(slot_i[:], slot_f[:]).then_inc(slots_ready, 1)
                    dve.wait_ge(e_done, 1)
                    link(dve.tensor_reduce(prob[:], below[:], AX_X, ALU.add))
                    link(dve.reciprocal(prob[:], prob[:]))

                    def step(n, s, stored):
                        if inside(n + 1):
                            dve.wait_ge(xt_done, n + 2)
                            dve.tensor_copy(xT[:, 1 - s, :], banks[5][:, 0:P]).then_inc(xT_ready, 1)
                            dve.tensor_copy(dest[:, bass.ds(n + 1, 1)], xin[:, 1 - s, P:ROW]).then_inc(dest_ready, 1)
                        if inside(n):
                            dve.wait_ge(up_ready, n + 1)
                            dve.tensor_tensor(gated[:, s, :], banks[2 * s + 1][:], up[:, s, :], ALU.mult
                                              ).then_inc(gated_ready, 1)
                        if inside(n - 2):
                            dve.wait_ge(y_done, n - 1)
                            if inside(n - 2, 2):
                                dve.wait_ge(y_out[s], (stored - 1 + layer * Y_USES[s]) * 16)
                            dve.tensor_copy(yout[:, s, :], banks[6][:, 0:P]).then_inc(y_ready, 1)

                    dve.wait_ge(xt_done, 1)
                    dve.tensor_copy(xT[:, 0, :], banks[5][:, 0:P]).then_inc(xT_ready, 1)
                    dve.tensor_copy(dest[:, 0:1], xin[:, 0, P:ROW]).then_inc(dest_ready, 1)
                    steps(dve, BLOCKS, step)
                    for g in range(NT // 4):
                        dve.wait_ge(y_in[g], 16)
                        for t in range(4 * g, 4 * g + 4):
                            dve.scalar_tensor_tensor(X[:, t, :], work[:, t, :], prob[:, t:t + 1], X[:, t, :],
                                                     ALU.mult, ALU.add).then_inc(x_done, 1)
                        if layer == 0:
                            dve.wait_ge(x_done, 4 * (g + 1))
                            for t in range(4 * g, 4 * g + 4):
                                dve.bn_stats(stats[:, t, :], X[:, t, :])

                @block.scalar
                def _(act):
                    act.wait_ge(shiftn_ready, 1)
                    for t in range(NT):
                        act.activation(H[:, t, :], X[:, t, :], ACT.Identity, bias=shiftn[:, t:t + 1],
                                       scale=rstd[:, t:t + 1]).then_inc(h_ready, 1)
                    act.wait_ge(e_in, 1)
                    act.activation(below[:], below[:], ACT.Exp).then_inc(e_done, 1)

                    def step(n, s, stored):
                        if inside(n):
                            act.wait_ge(up_done, n + 1)
                            act.activation(up[:, s, :], banks[2 * s][:], ACT.Silu).then_inc(up_ready, 1)
                        if inside(n - 1):
                            act.wait_ge(gt_done, n)
                            act.activation(gatedT[:, 1 - s, :], banks[4][:], ACT.Copy).then_inc(gT_ready, 1)

                    steps(act, BLOCKS, step)

                @block.tensor
                def _(pe):
                    pe.wait_ge(oh_ready, 1)
                    ohf = onehot_bf[:].rearrange("p t e -> p (t e)")
                    pe.matmul(banks[4][:, 0:NT * EXPERTS], ones_bf[:], ohf, start=True, stop=True)
                    pe.matmul(banks[3][:, 0:NT * EXPERTS], before_bf[:], ohf, start=True, stop=False)
                    for t in range(NT - 1):
                        last = pe.matmul(banks[3][:, (t + 1) * EXPERTS:NT * EXPERTS], ones_bf[:],
                                         onehot_bf[:, t:t + 1, :].broadcast_to([P, NT - 1 - t, EXPERTS]),
                                         start=False, stop=(t == NT - 2))
                    last.then_inc(r_done, 1)
                    pe.wait_ge(w1_in, 16)
                    pe.wait_ge(w2_in, 16)

                    def expert_of(n):
                        return pe.value_load(owner[0:1, bass.ds(n, 1)], min_val=0, max_val=EXPERTS - 1)

                    def enter(s, use):
                        pe.wait_ge(xin_ready[s], use * 16)
                        pe.transpose(banks[5][:, 0:P], xin[:, s, 0:P], ident).then_inc(xt_done, 1)

                    def step(n, s, stored):
                        if inside(n):
                            e = expert_of(n)
                            pe.wait_ge(xT_ready, n + 1)
                            for half in range(2):
                                last = pe.matmul(banks[2 * s + half][:], xT[:, s, :],
                                                 w1_sb[:, bass.ds(e, 1), half * FFN:(half + 1) * FFN]
                                                 .rearrange("p a n -> p (a n)"), start=True, stop=True)
                            last.then_inc(up_done, 1)
                        if inside(n + 1):
                            enter(1 - s, stored + 1 + s)
                        if inside(n - 1):
                            pe.wait_ge(gated_ready, n)
                            if inside(n - 1, 1):
                                pe.wait_ge(gT_ready, n - 1)
                            for j in range(FJ):
                                last = pe.transpose(banks[4][:, j * P:(j + 1) * P],
                                                    gated[:, 1 - s, j * P:(j + 1) * P], ident)
                            last.then_inc(gt_done, 1)
                        if inside(n - 2):
                            e = expert_of(n - 2)
                            pe.wait_ge(gT_ready, n - 1)
                            if inside(n - 2, 1):
                                pe.wait_ge(y_ready, n - 2)
                            for j in range(FJ):
                                last = pe.matmul(banks[6][:, 0:P], gatedT[:, s, j * P:(j + 1) * P],
                                                 w2_sb[:, bass.ds(e, 1), j, :].rearrange("p a n -> p (a n)"),
                                                 start=(j == 0), stop=(j == FJ - 1))
                            last.then_inc(y_done, 1)

                    enter(0, 1)
                    steps(pe, BLOCKS, step)

                @block.gpsimd
                def _(pool):
                    pool.wait_ge(pad_in, 16 * 2)
                    pool.wait_ge(slots_ready, 1)
                    pool.wait_ge(h_ready, NT)
                    for t in range(NT):
                        pool.indirect_dma_start(slots_dram[layer], bass.IndirectOffsetOnAxis(slot_i[:, t:t + 1], 0),
                                                rows[:, t, :], None).then_inc(scattered, 16)
                    for n in range(BLOCKS):
                        pool.wait_ge(y_ready, n + 1)
                        pool.indirect_dma_start(ys_dram, bass.IndirectOffsetOnAxis(dest[:, n:n + 1], 0),
                                                yout[:, n % 2, :], None).then_inc(y_out[n % 2], 16)

                @block.sync
                def _(sp):
                    sp.wait_ge(scattered, 16 * NT * (layer + 1))
                    for s in range(2):
                        sp.dma_start(xin[:, s, :], slots_dram[layer][s * P:(s + 1) * P, :]).then_inc(xin_ready[s], 16)

                    def step(n, s, stored):
                        if inside(n + 2):
                            sp.wait_ge(xt_done, n + 1)
                            sp.wait_ge(dest_ready, n + 1)
                            sp.dma_start(xin[:, s, :], slots_dram[layer][bass.ds((n + 2) * P, P), :]
                                         ).then_inc(xin_ready[s], 16)

                    steps(sp, BLOCKS, step)
                    for s in range(2):
                        sp.wait_ge(y_out[s], 16 * Y_USES[s] * (layer + 1))
                    for g in range(NT // 4):
                        sp.dma_start(work[:, 4 * g:4 * g + 4, :],
                                     ys_dram[4 * g * P:4 * (g + 1) * P, :].rearrange("(t p) c -> p t c", p=P)
                                     ).then_inc(y_in[g], 16)
                    if layer == 1:
                        outt = out.rearrange("b (t p) c -> p (b t) c", p=P)
                        for g in range(NT // 4):
                            sp.wait_ge(x_done, NT + 4 * (g + 1))
                            sp.dma_start(outt[:, 4 * g:4 * g + 4, :], X[:, 4 * g:4 * g + 4, :]).then_inc(final, 16)
                        sp.wait_ge(final, 16 * (NT // 4))

        def softmax_attention(stack, router):
            sb = own(stack)
            ctxb = sb("ctxb", [P, NT, P])
            vall = sb("vall", [P, BATCH, KT, P])
            hT_g = sb("b_hT", [P, 2, 4 * P])
            qst = sb("qst", [P, UNITS, HG, QH], BF16)
            kst = sb("kst", [P, BATCH, 2, SEQ], BF16)
            parts = sb("parts", [P, 2, 2, PARTS, QH], BF16)
            q_in = [sem(f"q_in{s}") for s in range(UNITS)]
            k_in = [sem(f"k_in{b}") for b in range(BATCH)]
            qsrc = qd.rearrange("m (g pair r d) t -> m g pair r d t", pair=2, r=2, d=DK)
            ksrc = kd.rearrange("m (g pair r d) t -> m g pair r d t", pair=2, r=2, d=DK)
            LOADS = 4
            NG = NT // 4
            low_ready = sem("b_lw")
            parts_out = [[sem(f"b_out{o}{s}") for s in range(2)] for o in range(2)]

            def stored(sp, b):
                for o in range(2):
                    for s in range(2):
                        sp.wait_ge(parts_out[o][s], 16 * PARTS * (b + 1))

            def store(sp, n):
                g, o = n // 2, n % 2
                sp.wait_ge(low_ready, n + 1)
                b, t0 = g // 2, g % 2 * QH
                m = 0
                for part in range(PARTS):
                    times = PARTS - part
                    dst = (qd, kd)[o][m:m + times, b * P:(b + 1) * P, t0:t0 + QH]
                    src = (parts[:, o, g % 2, part:part + 1, :].broadcast_to([P, times, QH]) if o == 0
                           else parts[:, o, g % 2, 0:times, :])
                    sp.dma_start(dst.rearrange("m c t -> c m t"), src).then_inc(parts_out[o][g % 2], 16)
                    m += times

            def load_q(sp, i, s):
                b, t0 = s // 2, s % 2 * QH
                for pair in range(2):
                    for r in range(2):
                        sp.dma_start(qst[PROWS * r:PROWS * (r + 1), s, 2 * pair + r, :],
                                     qsrc[:, bass.ds(i + b * HGROUPS, 1), pair, r, :, t0:t0 + QH]
                                     .rearrange("m g d t -> m (g d) t")).then_inc(q_in[s], 16)

            def load_k(sp, i, b):
                for pair in range(2):
                    for r in range(2):
                        sp.dma_start(kst[PROWS * r:PROWS * (r + 1), b, pair, :],
                                     ksrc[:, bass.ds(i + b * HGROUPS, 1), pair, r, :, :]
                                     .rearrange("m g d t -> m (g d) t")).then_inc(k_in[b], 16)

            def project(sb):
                full = sb("full", [P, 2, 2, QH])
                rest = sb("rest", [P, 2, 2, QH])
                link_d, var_ready, std_ready, h_ready = (sem(f"b_{n}") for n in ("link", "var", "std", "h"))
                t_done, t_copied, qk_done, v_done, head_ready, rest_ready, mid_ready, v_ready = (
                    sem(f"b_{n}") for n in ("t", "tc", "qk", "v", "hd", "rs", "md", "vr"))
                ones_ready, full_ready = sem("b_ones"), sem("b_full")

                with nc.Block() as block:
                    @block.gpsimd
                    def _(pool):
                        pool.memset(kst[SHIFT_ROW:P], 1.0).then_inc(ones_ready, 1)
                        pool.wait_ge(ones_ready, 1)
                        for s in range(UNITS):
                            pool.memset(qst[:, s], 0.0).then_inc(ones_ready, 1)

                    @block.vector
                    def _(dve):
                        link = linker(dve, link_d)
                        norm_stats(dve, link, var_ready, std_ready)
                        for t in range(NT):
                            normed(dve, H[:, t, :], X[:, t, :], t).then_inc(h_ready, 1)

                        def split(n):
                            g, o = n // 2, n % 2
                            if o == 0:
                                dve.wait_ge(qk_done, n + 2)
                                dve.tensor_scalar(full[:, 1, g % 2, :], banks[3 + 3 * (g % 2)], bcol[:, 1:2], None,
                                                  ALU.add).then_inc(full_ready, 1)
                            dve.wait_ge(head_ready, n + 1)
                            dve.tensor_tensor(rest[:, o, g % 2, :], full[:, o, g % 2, :],
                                              parts[:, o, g % 2, 0, :], ALU.subtract).then_inc(rest_ready, 1)

                        def low(n):
                            g, o = n // 2, n % 2
                            dve.wait_ge(mid_ready, n + 1)
                            dve.tensor_tensor(parts[:, o, g % 2, 2, :], rest[:, o, g % 2, :],
                                              parts[:, o, g % 2, 1, :], ALU.subtract).then_inc(low_ready, 1)

                        for n in range(2 * NG):
                            g = n // 2
                            split(n)
                            if n:
                                low(n - 1)
                            if n % 2:
                                dve.wait_ge(v_done, g + 1)
                                dve.tensor_tensor(vall[:, g // 2, g % 2 * 4:g % 2 * 4 + 4, :],
                                                  banks[4 + 3 * (g % 2)].rearrange("p (t c) -> p t c", t=4),
                                                  brow[:, 0:1, :].broadcast_to([P, 4, P]), ALU.add
                                                  ).then_inc(v_ready, 1)
                        low(2 * NG - 1)

                    @block.scalar
                    def _(act):
                        norm_sqrt(act, var_ready, std_ready)

                        def turned(g):
                            act.wait_ge(t_done, g + 1)
                            act.activation(hT_g[:, g % 2, :], banks[g % 2], ACT.Copy).then_inc(t_copied, 1)

                        def head(n):
                            g, o = n // 2, n % 2
                            act.wait_ge(qk_done, n + 1)
                            if g >= 2:
                                act.wait_ge(parts_out[o][g % 2], 16 * PARTS * (g // 2))
                                act.wait_ge(low_ready, n - 3)
                            if o == 0:
                                src = banks[2 + 3 * (g % 2)]
                                act.activation(full[:, 0, g % 2, :], src, ACT.Identity, bias=bcol[:, 0:1])
                                act.activation(parts[:, 0, g % 2, 0, :], src, ACT.Identity,
                                               bias=bcol[:, 0:1]).then_inc(head_ready, 1)
                            else:
                                act.wait_ge(full_ready, g + 1)
                                act.activation(parts[:, 1, g % 2, 0, :], full[:, 1, g % 2, :], ACT.Copy
                                               ).then_inc(head_ready, 1)

                        def middle(n):
                            g, o = n // 2, n % 2
                            act.wait_ge(rest_ready, n + 1)
                            act.activation(parts[:, o, g % 2, 1, :], rest[:, o, g % 2, :], ACT.Copy
                                           ).then_inc(mid_ready, 1)

                        turned(0)
                        for n in range(2 * NG):
                            if n % 2 and n // 2 + 1 < NG:
                                turned(n // 2 + 1)
                            head(n)
                            if n:
                                middle(n - 1)
                        middle(2 * NG - 1)

                    @block.tensor
                    def _(pe):
                        def turn(g):
                            pe.wait_ge(h_ready, 4 * g + 4)
                            for k in range(4):
                                last = pe.transpose(banks[g % 2][:, k * P:(k + 1) * P], H[:, 4 * g + k, :], ident)
                            last.then_inc(t_done, 1)

                        turn(0)
                        for g in range(NG):
                            if g + 1 < NG:
                                turn(g + 1)
                            pe.wait_ge(t_copied, g + 1)
                            base = 2 + 3 * (g % 2)
                            for o in range(2):
                                if g >= 2:
                                    pe.wait_ge(head_ready, 2 * (g - 2) + o + 1)
                                    if o:
                                        pe.wait_ge(full_ready, g - 1)
                                pe.matmul(banks[base + o], bw_sb[:, o, :], hT_g[:, g % 2, :], start=True, stop=True
                                          ).then_inc(qk_done, 1)
                            if g >= 2:
                                pe.wait_ge(v_ready, g - 1)
                            for k in range(4):
                                last = pe.matmul(banks[base + 2][:, k * P:(k + 1) * P],
                                                 hT_g[:, g % 2, k * P:(k + 1) * P], bw_sb[:, 2, :],
                                                 start=True, stop=True)
                            last.then_inc(v_done, 1)

                    @block.sync
                    def _(sp):
                        store(sp, 0)
                        store(sp, 1)
                        sp.wait_ge(ones_ready, 1 + UNITS)
                        sp.wait_ge(parts_out[0][0], 16 * PARTS)
                        load_q(sp, 0, 0)
                        store(sp, 2)
                        store(sp, 3)
                        stored(sp, 0)
                        load_k(sp, 0, 0)

            def attend(sb):
                vst = sb("vst", [P, BATCH, KT, HG, 32])
                probs = sb("probs", [P, 4, HG, QH])
                shift = sb("shift", [P, 2, QT, HG])
                shift_rest = sb("shift_rest", [P, QT, HG])
                once = sb("once", [P, QT, HG])
                shift_parts = sb("shift_parts", [P, QT, HG, PARTS], BF16)
                shift_rows = sb("shift_rows", [HG * PARTS, 2, QH], BF16)
                ctxT = sb("ctxT", [P, QH])
                rden = sb("b_rden", [P, 2, QT, HG])
                shift_in = [sem(f"shift_in{s}") for s in range(UNITS)]
                v_staged = [sem(f"v_staged{b}") for b in range(BATCH)]
                act_filled, act_drained, dve_filled, dve_drained, values_done = (
                    sem(f"at_{n}") for n in ("af", "ad", "df", "dd", "values"))
                shift_link, parts_ready = sem("sh_link"), sem("sh_parts")
                ctxT_ready, rden_ready, v_clear = (sem(f"cx_{n}") for n in ("T", "rden", "vclear"))

                ACT_RING, DVE_RING, VALUE_BANK = 3, 2, banks[7]
                MAX_TILES = QT * HG
                PER_STEP = MAX_TILES // KT
                PER_UNIT = KT * HG + 1

                def schedule(first, last):
                    for s in range(UNITS):
                        for kt in range(KT):
                            ahead = s + 1 if kt < KT // 2 else s + 2
                            tile = (kt + KT // 2) % KT * PER_STEP
                            for j in range(HG):
                                yield "score", s, kt, j
                                if kt == 1 and j == 1 and (s or not first):
                                    yield "context", s - 1, 0, 0
                                if j % 2 == 0 and not (last and ahead >= UNITS):
                                    yield "max", ahead, tile + j // 2, 0
                            if kt:
                                yield "values", s, kt - 1, 0
                            elif s or not first:
                                yield "values", s - 1, KT - 1, 0
                            if kt == 2 and (s or not first):
                                yield "turn", s - 1, 0, 0
                            if kt == 5 and not (last and s == UNITS - 1):
                                yield "rows", s + 1, 0, 0

                opening = [("max", 0, n, 0) for n in range(MAX_TILES)]
                opening += [("rows", 0, 0, 0)] + [("max", 1, n, 0) for n in range(MAX_TILES // 2)]
                closing = [("values", UNITS - 1, KT - 1, 0), ("context", UNITS - 1, 0, 0), ("turn", UNITS - 1, 0, 0)]

                def numbered(work, to_act, to_dve):
                    out, scored = [], {}
                    start = to_act
                    for kind, s, a, j in work:
                        if kind in ("score", "rows"):
                            out.append((kind, s, a, j, to_act))
                            to_act += 1
                            if kind == "score":
                                scored[s, a] = to_act
                        elif kind in ("max", "turn"):
                            out.append((kind, s, a, j, to_dve))
                            to_dve += 1
                        else:
                            out.append((kind, s, a, j, scored.get((s, a), start)))
                    return out, to_act, to_dve

                opening, to_act, to_dve = numbered(opening, 0, 0)
                first_group, to_act, to_dve = numbered(schedule(True, False), to_act, to_dve)
                middle_group, act_end, dve_end = numbered(schedule(False, False), to_act, to_dve)
                GROUP_ACT, GROUP_DVE = act_end - to_act, dve_end - to_dve
                assert GROUP_ACT % ACT_RING == 0 and GROUP_DVE % DVE_RING == 0
                last_group, act_end, dve_end = numbered(schedule(False, True), to_act + (HGROUPS - 2) * GROUP_ACT,
                                                        to_dve + (HGROUPS - 2) * GROUP_DVE)
                closing, _, _ = numbered(closing, act_end, dve_end)

                def in_group(work, i, repeat=1):
                    for kind, s, a, j, place in work:
                        size, ring = ((GROUP_DVE, DVE_RING) if kind in ("max", "turn") else (GROUP_ACT, ACT_RING))
                        slot = place % ring
                        bank = banks[slot] if ring == ACT_RING else psum[:, ACT_RING + 2 * slot:ACT_RING + 2 * slot + 2, :]
                        place = repeat * size + (place - size) if ring == DVE_RING else place + (repeat - 1) * size
                        yield kind, i + s // UNITS, s % UNITS, i * UNITS + s, a, j, place, bank

                def rounds(eng, step):
                    for w in in_group(opening, 0):
                        step(*w)
                    for w in in_group(first_group, 0):
                        step(*w)
                    with eng.Fori(1, HGROUPS - 1) as i:
                        for w in in_group(middle_group, i, i):
                            step(*w)
                    for w in in_group(last_group, HGROUPS - 1):
                        step(*w)
                    for w in in_group(closing, HGROUPS - 1):
                        step(*w)

                def positive(n):
                    return not isinstance(n, int) or n > 0

                with nc.Block() as block:
                    @block.sync
                    def _(sp):
                        def load_shift(count, s):
                            sp.wait_ge(act_drained, count)
                            for j in range(HG):
                                sp.dma_start(qst[SHIFT_ROW:ROWS, s, j, :],
                                             shift_rows[j * PARTS:(j + 1) * PARTS, s % 2, :]
                                             ).then_inc(shift_in[s], 16)

                        def group(i, last):
                            for s in range(UNITS):
                                u = i * UNITS + s
                                if not (last and s == UNITS - 1):
                                    load_shift(1 + u * PER_UNIT + 6 * HG + 1, (s + 1) % UNITS)
                                if not last:
                                    sp.wait_ge(values_done, u * KT + KT)
                                    if s % 2:
                                        load_k(sp, i + 1, s // 2)
                                    load_q(sp, i + 1, s)

                        load_q(sp, 0, 1)
                        for n in range(NG, 2 * NG):
                            store(sp, n)
                        stored(sp, 1)
                        load_k(sp, 0, 1)
                        load_q(sp, 0, 2)
                        load_q(sp, 0, 3)
                        load_shift(1, 0)
                        with sp.Fori(0, HGROUPS - 1) as i:
                            group(i, False)
                        group(HGROUPS - 1, True)

                    @block.gpsimd
                    def _(pool):
                        pool.memset(once[:], 1.0).then_inc(v_clear, 1)
                        pool.memset(vst[:], 0.0).then_inc(v_clear, 1)
                        pool.wait_ge(v_clear, 2)
                        pool.memset(vst[:, :, :, :, DK:DK + 1], 1.0).then_inc(v_clear, 1)

                        def stage(i, b):
                            pool.tensor_copy(vst[:, b, :, :, 0:DK],
                                             vall[:, b, :, bass.ds(i * HG * DK, HG * DK)]
                                             .rearrange("p t (h d) -> p t h d", h=HG)).then_inc(v_staged[b], 1)

                        def make_shift(u, s, place):
                            pool.wait_ge(dve_drained, place)
                            pool.tensor_tensor(shift_parts[:, :, :, 0], shift[:, s % 2], once[:], ALU.mult
                                               ).then_inc(shift_link, 1)
                            pool.wait_ge(shift_link, u * 3 + 1)
                            pool.tensor_tensor(shift_rest[:], shift[:, s % 2], shift_parts[:, :, :, 0],
                                               ALU.subtract).then_inc(shift_link, 1)
                            pool.wait_ge(shift_link, u * 3 + 2)
                            pool.tensor_tensor(shift_parts[:, :, :, 1], shift_rest[:], once[:], ALU.mult
                                               ).then_inc(shift_link, 1)
                            pool.wait_ge(shift_link, u * 3 + 3)
                            pool.tensor_tensor(shift_parts[:, :, :, 2], shift_rest[:], shift_parts[:, :, :, 1],
                                               ALU.subtract).then_inc(parts_ready, 1)

                        def group(i, first, last):
                            for s in range(UNITS):
                                u = i * UNITS + s
                                if not (last and s == UNITS - 1):
                                    make_shift(u + 1, (s + 1) % UNITS, 2 * MAX_TILES + u * (MAX_TILES + 1))
                                if s == 0 and not first:
                                    pool.wait_ge(values_done, u * KT)
                                    stage(i, 1)
                                if s == 2 and not last:
                                    pool.wait_ge(values_done, u * KT)
                                    stage(i + 1, 0)

                        pool.wait_ge(v_clear, 3)
                        for b in range(BATCH):
                            stage(0, b)
                        make_shift(0, 0, MAX_TILES)
                        group(0, True, False)
                        with pool.Fori(1, HGROUPS - 1) as i:
                            group(i, False, False)
                        group(HGROUPS - 1, False, True)
                        pool.tensor_tensor(X[:], X[:], brow[:, 3:4, :].broadcast_to([P, NT, P]), ALU.add)
                        pool.tensor_tensor(H[:], H[:], brow[:, 1:2, :].broadcast_to([P, NT, P]), ALU.add)

                    @block.vector
                    def _(dve):
                        def step(kind, i, s, u, a, j, place, bank):
                            if kind == "max":
                                dve.wait_ge(dve_filled, place + 1)
                                dve.tensor_reduce(shift[:, s % 2, a // HG, a % HG:a % HG + 1],
                                                  bank.rearrange("p k n -> p (k n)"), AX_X, ALU.max, negate=True
                                                  ).then_inc(dve_drained, 1)
                            elif kind == "turn":
                                dve.wait_ge(dve_filled, place + 1)
                                turned = bank[:, 0, :].rearrange("p (q h d) -> p q h d", q=QT, h=HG)
                                dve.reciprocal(rden[:, s % 2], turned[:, :, :, DK]).then_inc(rden_ready, 1)
                                dve.wait_ge(rden_ready, u + 1)
                                dve.tensor_tensor(ctxb[:, QT * s:QT * (s + 1), bass.ds(i * HG * DK, HG * DK)]
                                                  .rearrange("p q (h d) -> p q h d", h=HG),
                                                  turned[:, :, :, 0:DK],
                                                  rden[:, s % 2].unsqueeze(3).broadcast_to([P, QT, HG, DK]), ALU.mult
                                                  ).then_inc(dve_drained, 1)

                        rounds(dve, step)

                    @block.scalar
                    def _(act):
                        def step(kind, i, s, u, a, j, place, bank):
                            if kind == "score":
                                act.wait_ge(act_filled, place + 1)
                                if j == 0 and positive(u * KT + a - 3):
                                    act.wait_ge(values_done, u * KT + a - 3)
                                act.activation(probs[:, a % 4, j, :], bank, ACT.Exp, scale=SCALE
                                               ).then_inc(act_drained, 1)
                            elif kind == "rows":
                                act.wait_ge(act_filled, place + 1)
                                act.activation(shift_rows[:, s % 2, :], bank[0:HG * PARTS, :].bitcast(BF16)[:, 0:QH],
                                               ACT.Copy).then_inc(act_drained, 1)
                            elif kind == "context":
                                act.wait_ge(values_done, u * KT + KT)
                                act.activation(ctxT[:], VALUE_BANK, ACT.Copy).then_inc(ctxT_ready, 1)

                        rounds(act, step)

                    @block.tensor
                    def _(pe):
                        def step(kind, i, s, u, a, j, place, bank):
                            b = s // 2
                            if kind == "score":
                                if a == 0 and j == 0:
                                    pe.wait_ge(shift_in[s], (i + 1) * 16 * HG)
                                if positive(place - ACT_RING + 1):
                                    pe.wait_ge(act_drained, place - ACT_RING + 1)
                                pe.matmul(bank, kst[0:ROWS, b, j // 2, a * P:(a + 1) * P],
                                          qst[0:ROWS, s, j, :], start=True, stop=True
                                          ).then_inc(act_filled, 1)
                            elif kind == "max":
                                if a == 0:
                                    pe.wait_ge(q_in[s], (i + 1) * 16 * LOADS)
                                    pe.wait_ge(k_in[b], (i + 1) * 16 * LOADS)
                                if positive(place - DVE_RING + 1):
                                    pe.wait_ge(dve_drained, place - DVE_RING + 1)
                                qt, j = a // HG, a % HG
                                for half in range(2):
                                    last = pe.matmul(bank[:, half, :],
                                                     qst[0:SHIFT_ROW, s, j, qt * P:(qt + 1) * P],
                                                     kst[0:SHIFT_ROW, b, j // 2, half * 512:(half + 1) * 512],
                                                     start=True, stop=True)
                                last.then_inc(dve_filled, 1)
                            elif kind == "rows":
                                pe.wait_ge(parts_ready, u + 1)
                                if positive(place - ACT_RING + 1):
                                    pe.wait_ge(act_drained, place - ACT_RING + 1)
                                for qt in range(QT):
                                    last = pe.transpose(bank[0:HG * PARTS, :].bitcast(BF16)[:, qt * P:(qt + 1) * P],
                                                        shift_parts[:, qt, :, :].rearrange("p h n -> p (h n)"),
                                                        ident_bf[:])
                                last.then_inc(act_filled, 1)
                            elif kind == "turn":
                                pe.wait_ge(ctxT_ready, u + 1)
                                pe.wait_ge(dve_drained, place - DVE_RING + 1)
                                for qt in range(QT):
                                    last = pe.transpose(bank[:, 0, qt * P:(qt + 1) * P], ctxT[:, qt * P:(qt + 1) * P],
                                                        ident)
                                last.then_inc(dve_filled, 1)
                            elif kind == "values":
                                pe.wait_ge(act_drained, place)
                                if a == 0:
                                    pe.wait_ge(v_staged[b], i + 1)
                                    if positive(u):
                                        pe.wait_ge(ctxT_ready, u)
                                for j in range(HG):
                                    last = pe.matmul(VALUE_BANK[32 * j:32 * (j + 1), :], vst[:, b, a, j, :],
                                                     probs[:, a % 4, j, :], start=(a == 0), stop=(a == KT - 1))
                                last.then_inc(values_done, 1)

                        rounds(pe, step)

            def output():
                link_d, stats_done, var_ready, std_ready = (sem(f"o_{n}") for n in ("link", "stats", "var", "std"))
                t_done, t_copied, p_done, y_ready, n_ready = (sem(f"o_{n}") for n in ("t", "tc", "p", "y", "n"))
                shiftn_ready, gamma_done, x_ready = (sem(f"o_{n}") for n in ("shiftn", "gamma", "x"))
                with nc.Block() as block:
                    @block.vector
                    def _(dve):
                        link = linker(dve, link_d)
                        for g in range(NG):
                            dve.wait_ge(p_done, g + 1)
                            dve.tensor_tensor(work[:, 4 * g:4 * g + 4, :],
                                              banks[2 + g % 2].rearrange("p (t c) -> p t c", t=4),
                                              H[:, 4 * g:4 * g + 4, :], ALU.add).then_inc(y_ready, 1)
                            dve.wait_ge(y_ready, g + 1)
                            for t in range(4 * g, 4 * g + 4):
                                last = dve.bn_stats(stats[:, t, :], work[:, t, :])
                            last.then_inc(stats_done, 1)
                        dve.wait_ge(stats_done, NG)
                        norm_stats(dve, link, var_ready, std_ready)
                        dve.scalar_tensor_tensor(shiftn[:], mean[:], -1.0, rstd[:], ALU.mult, ALU.mult
                                                 ).then_inc(shiftn_ready, 1)
                        for g in range(NG):
                            dve.wait_ge(gamma_done, g + 1)
                            dve.tensor_tensor(X[:, 4 * g:4 * g + 4, :], X[:, 4 * g:4 * g + 4, :],
                                              H[:, 4 * g:4 * g + 4, :], ALU.add).then_inc(x_ready, 1)
                            dve.wait_ge(x_ready, g + 1)
                            for t in range(4 * g, 4 * g + 4):
                                last = dve.bn_stats(stats[:, t, :], X[:, t, :])
                            last.then_inc(router.stats_done, 1)
                        dve.wait_ge(router.stats_done, NG)
                        norm_stats(dve, link, router.var_ready, router.std_ready)

                    @block.gpsimd
                    def _(pool):
                        for g in range(NG):
                            pool.wait_ge(n_ready, 4 * (g + 1))
                            pool.tensor_tensor(H[:, 4 * g:4 * g + 4, :], work[:, 4 * g:4 * g + 4, :],
                                               brow[:, 2:3, :].broadcast_to([P, 4, P]), ALU.mult
                                               ).then_inc(gamma_done, 1)

                    @block.scalar
                    def _(act):
                        for g in range(NG):
                            act.wait_ge(t_done, g + 1)
                            act.activation(hT_g[:, g % 2, :], banks[g % 2], ACT.Copy).then_inc(t_copied, 1)
                        norm_sqrt(act, var_ready, std_ready)
                        act.wait_ge(shiftn_ready, 1)
                        for g in range(NG):
                            for t in range(4 * g, 4 * g + 4):
                                act.activation(work[:, t, :], work[:, t, :], ACT.Identity, bias=shiftn[:, t:t + 1],
                                               scale=rstd[:, t:t + 1]).then_inc(n_ready, 1)
                            if g >= 2:
                                router.on_act(act, g - 2)
                        router.on_act(act, NG - 2)
                        norm_sqrt(act, router.var_ready, router.std_ready)
                        router.on_act(act, NG - 1)

                    @block.tensor
                    def _(pe):
                        def turn(g):
                            for k in range(4):
                                last = pe.transpose(banks[g % 2][:, k * P:(k + 1) * P], ctxb[:, 4 * g + k, :], ident)
                            last.then_inc(t_done, 1)

                        turn(0)
                        for g in range(NG):
                            if g + 1 < NG:
                                turn(g + 1)
                            pe.wait_ge(t_copied, g + 1)
                            if g >= 2:
                                pe.wait_ge(y_ready, g - 1)
                            for k in range(4):
                                last = pe.matmul(banks[2 + g % 2][:, k * P:(k + 1) * P],
                                                 hT_g[:, g % 2, k * P:(k + 1) * P], bw_sb[:, 3, :],
                                                 start=True, stop=True)
                            last.then_inc(p_done, 1)
                        router.on_pe(pe, lambda g: range(4 * g, 4 * g + 4), lambda g: pe.wait_ge(x_ready, g + 1))

            with ExitStack() as inner:
                project(own(inner))
            with ExitStack() as inner:
                attend(own(inner))
            output()

        x_done, final = sem("x_done"), sem("final")
        router = Router(0)
        with ExitStack() as stack:
            linear_attention(own(stack), router)
        with ExitStack() as stack:
            experts(0, own(stack), router)
        router = Router(1)
        with ExitStack() as stack:
            softmax_attention(stack, router)
        with ExitStack() as stack:
            experts(1, own(stack), router)


_INS = ["L0_attn_a_x", "L0_attn_a_Wq", "L0_attn_a_Wk", "L0_attn_a_Wv", "L0_attn_a_Wo", "L0_attn_a_bo",
        "L0_attn_b_Wq", "L0_attn_b_bq", "L0_attn_b_Wk", "L0_attn_b_bk", "L0_attn_b_Wv", "L0_attn_b_bv",
        "L0_attn_b_Wo", "L0_attn_b_bo", "L0_attn_b_gamma", "L0_attn_b_beta", "L0_ffn_router_w",
        "L0_ffn_router_b", "L0_ffn_w1", "L0_ffn_w2"]


def kernel(**inputs):
    import numpy as np
    import concourse.bacc as bacc
    from concourse.bass_utils import run_bass_kernel_spmd

    nc = bacc.Bacc("TRN2", target_bir_lowering=False, num_devices=1)
    arrays = {name: np.ascontiguousarray(inputs[name]) for name in _INS}
    arrays["shape_tables"] = constants()
    args = [nc.dram_tensor(name, a.shape, mybir.dt.from_np(a.dtype), kind="ExternalInput").ap()
            for name, a in arrays.items()]
    out = nc.dram_tensor("out", inputs["L0_attn_a_x"].shape, F32, kind="ExternalOutput").ap()
    hybrid_layer(nc, *args, out)
    r = run_bass_kernel_spmd(nc, [arrays], core_ids=[0])
    return r.results[0]["out"]
```
